# Optimizing a Trainium2 kernel written in Bass

```python
import numpy as np
import jax
import jax.numpy as jnp

def _softmax(x, axis=-1):
    return jax.nn.softmax(x, axis=axis)

def _gelu(x):
    return jax.nn.gelu(x, approximate=True)

def _silu(x):
    return jax.nn.silu(x)

def _sigmoid(x):
    return jax.nn.sigmoid(x)

def _layernorm(x, axis=-1, eps=1e-05):
    m = jnp.mean(x, axis=axis, keepdims=True)
    v = jnp.var(x, axis=axis, keepdims=True)
    return (x - m) / jnp.sqrt(v + eps)

def _scatter_add(tgt, idx, src, axis=0):
    return tgt.at[idx].add(src)

def _segment_sum(src, seg, n):
    return jax.ops.segment_sum(src, seg, n)
kernel_name = 'mk_sandwich_d1_jaxref_r8_ee52db'

def setup_inputs(seed: int=0):
    np.random.seed(seed)
    _w = jnp.asarray

    def _L0_attn_setup():
        import jax, jax.numpy as jnp
        import numpy as np
        D_MODEL = 128
        N_HEADS = 16
        D_HEAD = D_MODEL // N_HEADS
        key = jax.random.key(seed)
        ks = jax.random.split(key, 5)
        B, S = (1, 256)
        x = jax.random.normal(ks[0], (B, S, D_MODEL), dtype=jnp.float32)
        lim = float(np.sqrt(6.0 / (2 * D_MODEL)))

        def w(k):
            return jax.random.uniform(k, (D_MODEL, D_MODEL), jnp.float32, -lim, lim)
        return {'x': x, 'Wq': w(ks[1]), 'bq': jnp.zeros((D_MODEL,), jnp.float32), 'Wk': w(ks[2]), 'bk': jnp.zeros((D_MODEL,), jnp.float32), 'Wv': w(ks[3]), 'bv': jnp.zeros((D_MODEL,), jnp.float32), 'Wo': w(ks[4]), 'bo': jnp.zeros((D_MODEL,), jnp.float32)}
    _L0_attn_in = _L0_attn_setup()

    def _L0_ffn_setup():
        import jax, jax.numpy as jnp
        import numpy as np
        NUM_EXPERTS = 8
        TOP_K = 2
        key = jax.random.key(seed)
        ks = jax.random.split(key, 6)
        B, S, D, F = (2, 256, 128, 512)
        E = NUM_EXPERTS
        sd = 1.0 / np.sqrt(D)
        sf = 1.0 / np.sqrt(F)
        return {'x': jax.random.normal(ks[0], (B, S, D), dtype=jnp.float32), 'gate_w': jax.random.normal(ks[1], (E, D), dtype=jnp.float32) * sd, 'w1': jax.random.uniform(ks[2], (F, E, D), dtype=jnp.float32, minval=-sd, maxval=sd), 'b1': jax.random.uniform(ks[3], (E, F), dtype=jnp.float32, minval=-sd, maxval=sd), 'w2': jax.random.uniform(ks[4], (D, E, F), dtype=jnp.float32, minval=-sf, maxval=sf), 'b2': jax.random.uniform(ks[5], (E, D), dtype=jnp.float32, minval=-sf, maxval=sf)}
    _L0_ffn_in = _L0_ffn_setup()
    _d = {'L0_attn_x': _L0_attn_in['x'], 'L0_attn_Wq': _L0_attn_in['Wq'], 'L0_attn_bq': _L0_attn_in['bq'], 'L0_attn_Wk': _L0_attn_in['Wk'], 'L0_attn_bk': _L0_attn_in['bk'], 'L0_attn_Wv': _L0_attn_in['Wv'], 'L0_attn_bv': _L0_attn_in['bv'], 'L0_attn_Wo': _L0_attn_in['Wo'], 'L0_attn_bo': _L0_attn_in['bo'], 'L0_ffn_gate_w': _L0_ffn_in['gate_w'], 'L0_ffn_w1': _L0_ffn_in['w1'], 'L0_ffn_b1': _L0_ffn_in['b1'], 'L0_ffn_w2': _L0_ffn_in['w2'], 'L0_ffn_b2': _L0_ffn_in['b2']}
    _x0 = _d['L0_attn_x']
    _d['L0_attn_x'] = jax.random.normal(jax.random.fold_in(jax.random.key(seed), 1), (16, 512, 128), dtype=_x0.dtype)
    del _x0
    return _d

def reference(L0_attn_x, L0_attn_Wq, L0_attn_bq, L0_attn_Wk, L0_attn_bk, L0_attn_Wv, L0_attn_bv, L0_attn_Wo, L0_attn_bo, L0_ffn_gate_w, L0_ffn_w1, L0_ffn_b1, L0_ffn_w2, L0_ffn_b2):

    def _L0_attn_ref(x, Wq, bq, Wk, bk, Wv, bv, Wo, bo):
        import jax, jax.numpy as jnp
        import numpy as np
        D_MODEL = 128
        N_HEADS = 16
        D_HEAD = D_MODEL // N_HEADS
        B, S, _ = x.shape
        H, d = (N_HEADS, D_HEAD)
        q = x @ Wq.T + bq
        k = x @ Wk.T + bk
        v = x @ Wv.T + bv

        def to_z(t):
            return t.reshape(B, S, H, d).transpose(0, 2, 1, 3).reshape(B * H, S, d)
        q = jax.nn.softplus(to_z(q))
        k = jax.nn.softplus(to_z(k))
        v = to_z(v)
        kv = jnp.cumsum(k[:, :, :, None] * v[:, :, None, :], axis=1)
        k1 = jnp.cumsum(k, axis=1)
        num = jnp.einsum('zsD,zsDe->zse', q, kv)
        den = jnp.sum(q * k1, axis=-1, keepdims=True)
        out = num / den
        out = out.reshape(B, H, S, d).transpose(0, 2, 1, 3).reshape(B, S, H * d)
        return out @ Wo.T + bo

    def _L0_ffn_ref(x, gate_w, w1, b1, w2, b2):
        import jax, jax.numpy as jnp
        import numpy as np
        NUM_EXPERTS = 8
        TOP_K = 2
        logits = jnp.einsum('bsd,ed->bse', x, gate_w)
        probs = jax.nn.softmax(logits, axis=-1)
        topk_probs, topk_idx = jax.lax.top_k(probs, TOP_K)
        oh = jax.nn.one_hot(topk_idx, NUM_EXPERTS, dtype=x.dtype)
        h = jnp.einsum('bsd,fed,bske->bskf', x, w1, oh)
        h = h + jnp.take(b1, topk_idx, axis=0)
        h = jax.nn.gelu(h)
        y = jnp.einsum('bskf,def,bske->bskd', h, w2, oh)
        y = y + jnp.take(b2, topk_idx, axis=0)
        out = jnp.sum(y * topk_probs[..., None], axis=-2)
        return out
    x = L0_attn_x
    x = x + _layernorm(_L0_attn_ref(_layernorm(x, axis=-1), L0_attn_Wq, L0_attn_bq, L0_attn_Wk, L0_attn_bk, L0_attn_Wv, L0_attn_bv, L0_attn_Wo, L0_attn_bo), axis=-1)
    x = x + _layernorm(_L0_ffn_ref(_layernorm(x, axis=-1), L0_ffn_gate_w, L0_ffn_w1, L0_ffn_b1, L0_ffn_w2, L0_ffn_b2), axis=-1)
    return x

_drawn_inputs = setup_inputs


def setup_inputs(seed=0):
    import zlib

    import numpy as np

    out = dict(_drawn_inputs(seed))
    spreads = {'L0_attn_bq': (0.0, 0.1),
     'L0_attn_bk': (0.0, 0.1),
     'L0_attn_bv': (0.0, 0.1),
     'L0_attn_bo': (0.0, 0.1)}
    factors = {}
    for name, (base, spread) in spreads.items():
        noise = np.random.default_rng([zlib.crc32(name.encode()), seed]).standard_normal(out[name].shape)
        drawn = base * np.exp(spread * noise) if base else spread * noise
        out[name] = jnp.asarray(drawn.astype(out[name].dtype))
    for name, factor in factors.items():
        out[name] = (out[name] * factor).astype(out[name].dtype)
    return out
```

```python
from contextlib import ExitStack

import concourse.bass as bass
from concourse import mybir

F32 = mybir.dt.float32
BF16 = mybir.dt.bfloat16
I32 = mybir.dt.int32
U32 = mybir.dt.uint32
ALU = mybir.AluOpType
ACT = mybir.ActivationFunctionType
AX = mybir.AxisListType.X

P = 128
B, S, D = 16, 512, 128
H, DH = 16, 8
NT = S // P
N = B * S
E, FF = 8, 512
FC = FF // P
DEN = DH + 1
HV = H * DEN
T = 256
CAP = N + T
MOE_TILES = (2 * N + E * (T - 1)) // T
RW = 132
WW = 2 * FF + FC + D + 2
EPS = 1e-5
OFFSETS = dict(E=0, F=1, M=2, O=3, R=4, S=5)
STEPS = B + 5


def wait(eng, sem, value):
    if isinstance(value, int) and value <= 0:
        return
    eng.wait_ge(sem, value)


def build(nc, x, wqkvT, woT, gateT, bqk, bv, bo, wexp, ident, tri, stri, mask, consts, pad, out):
    bucket = nc.dram_tensor("bucket", (E * CAP + T, RW), F32, kind="Internal").ap()
    ychoice = nc.dram_tensor("ychoice", (2 * N, D), F32, kind="Internal").ap()
    x_v = x.rearrange("b (c p) d -> p (b c) d", p=P)
    out_v = out.rearrange("b (c p) d -> p (b c) d", p=P)
    y_v = ychoice.rearrange("(k t p) d -> k p t d", k=2, p=P)

    with ExitStack() as ctx:
        def sb(name, shape, dt=F32):
            return ctx.enter_context(nc.sbuf_tensor(name, shape, dt))

        def ps(name, shape, dt=F32):
            return ctx.enter_context(nc.psum_tensor(name, shape, dt))

        def sem(name):
            return ctx.enter_context(nc.semaphore(name))

        def pair(name):
            return [sem(f"{name}{k}") for k in range(2)]

        w_qkv = sb("w_qkv", [P, 3 * D])
        w_o = sb("w_o", [P, D])
        w_gate = sb("w_gate", [P, E])
        b_qk = sb("b_qk", [P, 2])
        b_v = sb("b_v", [P, 1])
        b_o = sb("b_o", [1, D])
        attn_bias = sb("attn_bias", [1, D])
        idn = sb("idn", [P, P])
        tri_s = sb("tri_s", [P, P])
        tri_strict = sb("tri_strict", [P, P])
        tri_b = sb("tri_b", [P, P], BF16)
        ones_b = sb("ones_b", [P, P], BF16)
        ones_row = sb("ones_row", [1, P])
        head_mask = sb("head_mask", [P, HV])
        con = sb("con", [P, consts.shape[1]])
        eps_t = sb("eps_t", [P, 1])
        W = sb("W", [P, E, WW])
        pad_rows = sb("pad_rows", [P, 2 * RW])
        xe = [sb(f"xe{k}", [P, NT, D]) for k in range(2)]
        xr = [sb(f"xr{k}", [P, NT, D]) for k in range(2)]
        xn = [sb(f"xn{k}", [P, NT, D]) for k in range(2)]
        xnT = sb("xnT", [P, S])
        f_abs = sb("f_abs", [P, 2 * S])
        f_exp = sb("f_exp", [P, 2 * S])
        f_ln = sb("f_ln", [P, 2 * S])
        f_relu = sb("f_relu", [P, 2 * S])
        qkT = [sb(f"qkT{k}", [P, 2 * S]) for k in range(2)]
        qk = [sb(f"qk{k}", [P, NT, 2 * D]) for k in range(2)]
        vx = [sb(f"vx{k}", [P, NT, HV]) for k in range(2)]
        kv = [sb(f"kv{k}", [P, H * DH * DH]) for k in range(2)]
        prod = [sb(f"prod{k}", [P, H, DH, DEN]) for k in range(2)]
        num = [sb(f"num{k}", [P, H, DEN]) for k in range(2)]
        tot = [sb(f"tot{k}", [P, H, DEN]) for k in range(2)]
        rden = [sb(f"rden{k}", [P, H]) for k in range(2)]
        state = [sb(f"state{k}", [P, HV]) for k in range(2)]
        o = [sb(f"o{k}", [P, NT, D]) for k in range(2)]
        oT = sb("oT", [P, S])
        an = sb("an", [P, NT, D])
        x1 = [sb(f"x1{k}", [P, NT, D]) for k in range(2)]
        rows = [sb(f"rows{k}", [P, NT, RW]) for k in range(2)]
        xn2T = sb("xn2T", [P, S])
        logit = sb("logit", [P, NT, E])
        top = sb("top", [P, NT, E])
        topi = sb("topi", [P, NT, E], U32)
        topf = sb("topf", [P, NT, 2])
        dtop = sb("dtop", [P, NT, E])
        etop = sb("etop", [P, NT, E])
        zsum = sb("zsum", [P, NT])
        rz = sb("rz", [P, NT])
        hot = sb("hot", [P, NT, 2, E])
        hot_b = sb("hot_b", [P, NT, E], BF16)
        base = sb("base", [P, E])
        pos = sb("pos", [P, NT, E])
        psel = sb("psel", [P, NT, 2, E])
        slotf = sb("slotf", [P, NT * 2])
        slot = [sb(f"slot{k}", [P, NT * 2], I32) for k in range(2)]
        token = sb("token", [P, NT])
        st = {k: sb(f"st_{k}", [P, NT, 6]) for k in "earc"}
        mv = {k: sb(f"mv_{k}", [P, NT, 2]) for k in "earc"}
        nw = {k: sb(f"nw_{k}", [P, 6, NT]) for k in "earc"}
        x1_all = sb("x1_all", [P, B * NT, D])
        prob_all = sb("prob_all", [P, B * NT, 2])
        cnt = sb("cnt", [P, E])
        cmp32 = sb("cmp32", [P, E, 32])
        ntile = sb("ntile", [P, E])
        trie = sb("trie", [P, E, E])
        tend = sb("tend", [P, E])
        ge = sb("ge", [P, MOE_TILES, E])
        gen = sb("gen", [P, MOE_TILES, E])
        ex_of = sb("ex_of", [P, MOE_TILES])
        t_start = sb("t_start", [P, MOE_TILES])
        row_of = sb("row_of", [P, MOE_TILES])
        row_b = sb("row_b", [P, MOE_TILES])
        ex_min = sb("ex_min", [P, MOE_TILES])
        row_i = sb("row_i", [P, MOE_TILES], I32)
        ex_i = sb("ex_i", [P, MOE_TILES], I32)
        end_i = sb("end_i", [P, E], I32)
        xg = [sb(f"xg{k}", [P, 2, RW]) for k in range(2)]
        we = [sb(f"we{k}", [P, WW]) for k in range(2)]
        xgT = [sb(f"xgT{k}", [P, T]) for k in range(2)]
        hid = [sb(f"hid{k}", [P, FC, T]) for k in range(2)]
        yv = [sb(f"yv{k}", [P, 2, D]) for k in range(2)]
        second = [sb(f"second{k}", [P, 2]) for k in range(2)]
        dest = [sb(f"dest{k}", [P, 2], I32) for k in range(2)]
        y0, y1 = xe, xr
        yp, ys, yn, fin = xn, x1, o, [rows[k][:, :, 0:D] for k in range(2)]
        pc = [sb(f"pc{k}", [P, NT * 2]) for k in range(2)]

        kv_ps = [ps(f"kv_ps{k}", [P, 512]) for k in range(2)]
        small = ps("small", [P, 512])
        st_ps = ps("st_ps", [P, 512])
        qk_ps = ps("qk_ps", [P, 1024])
        xv_ps = ps("xv_ps", [P, 512])
        out_ps = ps("out_ps", [P, 512])
        k1_ps = small[:, 0:D]
        inter_ps = small[:, D:D + HV]
        logit_ps = out_ps[:, 0:NT * E].rearrange("p (c e) -> p c e", c=NT)
        rank_ps = xv_ps[:, 0:NT * E].rearrange("p (c e) -> p c e", c=NT)
        count_ps = xv_ps[:, NT * E:NT * E + E]
        gT_ps, y_ps = (xv_ps, st_ps), (out_ps, small)

        iota8 = con[:, 0:E]
        ecap = con[:, E:2 * E]
        m256 = con[:, 16:48]
        lower = con[:, 48:48 + E * E].rearrange("p (a b) -> p a b", a=E)
        tnum = con[:, 112:112 + MOE_TILES]
        tok0 = con[:, 183:183 + NT]

        consts_in, w_in = sem("consts_in"), sem("w_in")
        init, init_a = sem("init"), sem("init_a")
        bias_mm, bias_row = sem("bias_mm"), sem("bias_row")
        xe_in, xr_in = pair("xe_in"), pair("xr_in")
        stat = {k: sem(f"stat_{k}") for k in "earc"}
        lnexp = {k: sem(f"lnexp_{k}") for k in "earc"}
        newton = {k: sem(f"newton_{k}") for k in "earc"}
        xn_done = sem("xn_done")
        xnT_mm, xnT_sb = sem("xnT_mm"), sem("xnT_sb")
        qk_mm, v_mm, v_sb = sem("qk_mm"), sem("v_mm"), sem("v_sb")
        soft_a, soft_sum = sem("soft_a"), sem("soft_sum")
        qkt_mm, qk_sb = sem("qkt_mm"), sem("qk_sb")
        outer, cum, k1_mm = sem("outer"), sem("cum"), sem("k1_mm")
        state_mm, state_sb = sem("state_mm"), sem("state_sb")
        m_prod, m_red, m_tot, m_rden, o_done = (sem(n) for n in ("m_prod", "m_red", "m_tot", "m_rden", "o_done"))
        oT_mm, oT_sb, a_mm, an_done, x1_done = (sem(n) for n in ("oT_mm", "oT_sb", "a_mm", "an_done", "x1_done"))
        x1_kept = pair("x1_kept")
        rows_done = sem("rows_done")
        x2T_mm, x2T_sb, logit_mm, route, etop_done, rank_mm = (
            sem(n) for n in ("x2T_mm", "x2T_sb", "logit_mm", "route", "etop_done", "rank_mm"))
        meta, slots, scattered = sem("meta"), sem("slots"), pair("scattered")
        table, pads_in = sem("table"), sem("pads_in")
        xg_in, we_done = pair("xg_in"), sem("we_done")
        gT_mm, gT_sb, h_mm, h_done, y_mm, y_done, dest_a, dest_done = (
            sem(n) for n in ("gT_mm", "gT_sb", "h_mm", "h_done", "y_mm", "y_done", "dest_a", "dest_done"))
        y_sent = pair("y_sent")
        y_in, pc_done, yp_done, ys_done, yn_done, fin_done = (
            pair("y_in"), sem("pc_done"), sem("yp_done"), sem("ys_done"), sem("yn_done"), sem("fin_done"))
        stored = pair("stored")

        n_const = 12 * 16
        block = ctx.enter_context(nc.Block())

        def hold(eng, *waits):
            known = [(s, v if isinstance(v, int) else eng.to_reg(v)) for s, v in waits]
            eng.wait_ge(consts_in, n_const)
            for s, v in known:
                wait(eng, s, v)

        def tile_of(eng, j):
            return j * NT if isinstance(j, int) else eng.snap(j * NT)

        def stages(i, t, u):
            found = {}
            for name, lag in OFFSETS.items():
                j = i - lag
                if isinstance(i, int) and not 0 <= j < B:
                    continue
                found[name] = (j, (u - lag) % 2, t + (u - lag) // 2)
            return found

        def run_steps(eng, step):
            for i in range(6):
                step(stages(i, i // 2, i % 2))
            with eng.Fori(3, B // 2) as t:
                for u in range(2):
                    step(stages(2 * t + u, t, u))
            for i in range(B, STEPS):
                step(stages(i, i // 2, i % 2))

        def h_ps(p, f):
            bank = (kv_ps[f // 2] if p == 0 else qk_ps[:, (f // 2) * 512:(f // 2 + 1) * 512])
            return bank[:, (f % 2) * T:(f % 2 + 1) * T]

        @block.sync
        def _(sp):
            for dst, src in ((idn, ident), (w_qkv, wqkvT), (b_qk, bqk), (tri_s, tri), (head_mask, mask),
                             (con, consts), (w_o, woT), (w_gate, gateT), (b_v, bv), (b_o, bo),
                             (tri_strict, stri), (pad_rows, pad)):
                sp.dma_start(dst[:], src).then_inc(consts_in, 16)

            def step(at):
                if "E" in at:
                    j, p, r = at["E"]
                    first = tile_of(sp, j)
                    wait(sp, xn_done, (j - 1) * NT)
                    sp.dma_start(xe[p][:], x_v[:, bass.ds(first, NT), :]).then_inc(xe_in[p], 16)
                if "M" in at:
                    j, p, r = at["M"]
                    first = tile_of(sp, j)
                    wait(sp, x1_done, j - 1)
                    sp.dma_start(xr[p][:], x_v[:, bass.ds(first, NT), :]).then_inc(xr_in[p], 16)
                if "O" in at:
                    j, p, r = at["O"]
                    first = tile_of(sp, j)
                    wait(sp, x1_done, j + 1)
                    sp.dma_start(x1_all[:, bass.ds(first, NT), :], x1[p][:]).then_inc(x1_kept[p], 16)

            run_steps(sp, step)
            sp.wait_ge(table, 20)
            for e in range(E):
                end = sp.value_load(end_i[0:1, e:e + 1], min_val=e * CAP, max_val=e * CAP + N)
                sp.dma_start(bucket[bass.ds(end, T), :].rearrange("(p j) w -> p (j w)", p=P), pad_rows[:]
                             ).then_inc(pads_in, 16)
            sp.dma_start(bucket[E * CAP:E * CAP + T, :].rearrange("(p j) w -> p (j w)", p=P), pad_rows[:]
                         ).then_inc(pads_in, 16)
            sp.wait_ge(pads_in, 16 * (E + 1))
            for p in range(2):
                sp.wait_ge(scattered[p], (B // 2) * 2 * NT * 16)

            def load_rows(i, p):
                row = sp.value_load(row_i[0:1, bass.ds(i, 1)], min_val=0, max_val=E * CAP)
                wait(sp, gT_mm, i - 1)
                wait(sp, dest_done, i - 1)
                sp.dma_start(xg[p][:].rearrange("p j w -> p (j w)"),
                             bucket[bass.ds(row, T), :].rearrange("(p j) w -> p (j w)", p=P)).then_inc(xg_in[p], 16)

            for i in range(2):
                load_rows(i, i)
            with sp.Fori(1, MOE_TILES // 2) as t:
                for p in range(2):
                    load_rows(2 * t + p, p)
            load_rows(MOE_TILES - 1, 0)
            sp.wait_ge(y_sent[0], (MOE_TILES + 1) // 2 * 32)
            sp.wait_ge(y_sent[1], MOE_TILES // 2 * 32)

            def load_y(j, p):
                first = tile_of(sp, j)
                wait(sp, ys_done, (j - 1) * NT)
                for k, y in enumerate((y0, y1)):
                    sp.dma_start(y[p][:], y_v[k, :, bass.ds(first, NT), :]).then_inc(y_in[p], 16)

            def store(j, p):
                first = tile_of(sp, j)
                sp.wait_ge(fin_done, j + 1)
                sp.dma_start(out_v[:, bass.ds(first, NT), :], fin[p]).then_inc(stored[p], 16)

            for j in range(2):
                load_y(j, j)
            with sp.Fori(1, B // 2) as t:
                for p in range(2):
                    load_y(2 * t + p, p)
                    store(2 * t + p - 2, p)
            for j in range(B - 2, B):
                store(j, j % 2)
            for p in range(2):
                sp.wait_ge(stored[p], B // 2 * 16)

        def layer_norm_act(act, key, j):
            act.wait_ge(stat[key], j * 2 * NT + 2 * NT)
            act.activation(nw[key][:, 0, :], mv[key][:, :, 1], ACT.Ln, bias=eps_t[:, 0:1]).then_inc(lnexp[key], 1)
            act.wait_ge(lnexp[key], j * 2 + 1)
            act.activation(nw[key][:, 1, :], nw[key][:, 0, :], ACT.Exp, scale=-0.5).then_inc(lnexp[key], 1)

        def layer_norm_stats(v, key, j, tiles, first, waits):
            for c in range(NT):
                if c == 0:
                    waits()
                v.bn_stats(st[key][:, c, :], tiles(c)).then_inc(stat[key], 1)
            hold(v, (stat[key], j * 2 * NT + NT))
            for c in range(NT):
                v.bn_aggr(mv[key][:, c, :], st[key][:, c, :]).then_inc(stat[key], 1)

        def layer_norm_newton(v, key, j):
            a = nw[key]
            v.wait_ge(lnexp[key], j * 2 + 2)
            v.scalar_tensor_tensor(a[:, 2, :], mv[key][:, :, 1], EPS, a[:, 1, :], ALU.add, ALU.mult
                                   ).then_inc(newton[key], 1)
            v.wait_ge(newton[key], j * 4 + 1)
            v.scalar_tensor_tensor(a[:, 3, :], a[:, 2, :], -0.5, a[:, 1, :], ALU.mult, ALU.mult
                                   ).then_inc(newton[key], 1)
            v.wait_ge(newton[key], j * 4 + 2)
            v.scalar_tensor_tensor(a[:, 4, :], a[:, 3, :], 1.5, a[:, 1, :], ALU.add, ALU.mult
                                   ).then_inc(newton[key], 1)
            v.wait_ge(newton[key], j * 4 + 3)
            v.scalar_tensor_tensor(a[:, 5, :], mv[key][:, :, 0], -1.0, a[:, 4, :], ALU.mult, ALU.mult
                                   ).then_inc(newton[key], 1)

        @block.scalar
        def _(act):
            act.dma_start(W[:], wexp).then_inc(w_in, 16)
            act.wait_ge(init, 5)
            act.wait_ge(bias_mm, 1)
            act.activation(attn_bias[:], st_ps[0:1, 0:D], ACT.Copy).then_inc(init_a, 1)

            def step(at):
                if "F" in at:
                    j, p, r = at["F"]
                    act.wait_ge(xnT_mm, j + 1)
                    wait(act, v_mm, j)
                    act.activation(xnT[:], xv_ps[:], ACT.Copy).then_inc(xnT_sb, 1)
                if "R" in at:
                    j, p, r = at["R"]
                    act.wait_ge(x2T_mm, j + 1)
                    wait(act, logit_mm, j)
                    act.activation(xn2T[:], out_ps[:], ACT.Copy).then_inc(x2T_sb, 1)
                if "F" in at:
                    j, p, r = at["F"]
                    act.wait_ge(qk_mm, j + 1)
                    wait(act, soft_sum, j)
                    for k in range(2):
                        act.activation(f_abs[:, k * S:(k + 1) * S], qk_ps[:, k * S:(k + 1) * S], ACT.Abs,
                                       bias=b_qk[:, k:k + 1]).then_inc(soft_a, 1)
                    for k in range(2):
                        act.activation(f_relu[:, k * S:(k + 1) * S], qk_ps[:, k * S:(k + 1) * S], ACT.Relu,
                                       bias=b_qk[:, k:k + 1]).then_inc(soft_a, 1)
                    act.wait_ge(soft_a, j * 6 + 2)
                    act.activation(f_exp[:], f_abs[:], ACT.Exp, scale=-1.0).then_inc(soft_a, 1)
                    act.wait_ge(soft_a, j * 6 + 5)
                    act.activation(f_ln[:], f_exp[:], ACT.Ln, bias=1.0).then_inc(soft_a, 1)
                    act.wait_ge(v_mm, j + 1)
                    wait(act, outer, (j - 1) * NT)
                    wait(act, state_mm, (j - 1) * (NT - 1))
                    act.activation(vx[p][:].rearrange("p c (h w) -> p c h w", w=DEN)[:, :, :, 0:DH],
                                   xv_ps[:].rearrange("p (c h e) -> p c h e", c=NT, h=H), ACT.Copy).then_inc(v_sb, 1)
                if "O" in at:
                    j, p, r = at["O"]
                    act.wait_ge(oT_mm, j + 1)
                    wait(act, a_mm, j)
                    act.activation(oT[:], out_ps[:], ACT.Copy).then_inc(oT_sb, 1)
                if "R" in at:
                    j, p, r = at["R"]
                    act.wait_ge(route, j * 13 + 9)
                    wait(act, route, (j - 1) * 13 + 13)
                    act.activation(etop[:], dtop[:], ACT.Exp).then_inc(etop_done, 1)
                if "F" in at:
                    j, p, r = at["F"]
                    act.wait_ge(qkt_mm, j + 1)
                    wait(act, cum, (j - 1) * NT)
                    wait(act, m_prod, (j - 1) * NT * 3)
                    for k in range(2):
                        act.activation(qk[p][:, 2 * k:2 * k + 2, :].rearrange("p c w -> p (c w)"),
                                       qk_ps[:, k * 512:(k + 1) * 512], ACT.Copy).then_inc(qk_sb, 1)
                if "O" in at:
                    j, p, r = at["O"]
                    layer_norm_act(act, "a", j)
                    act.wait_ge(newton["a"], j * 4 + 4)
                    wait(act, x1_done, j)
                    for c in range(NT):
                        act.activation(an[:, c, :], out_ps[:, c * D:(c + 1) * D], ACT.Identity,
                                       bias=nw["a"][:, 5, c:c + 1], scale=nw["a"][:, 4, c:c + 1]).then_inc(an_done, 1)
                if "E" in at:
                    j, p, r = at["E"]
                    layer_norm_act(act, "e", j)
                    act.wait_ge(newton["e"], j * 4 + 4)
                    wait(act, xnT_mm, j - 1)
                    for c in range(NT):
                        act.activation(xn[p][:, c, :], xe[p][:, c, :], ACT.Identity,
                                       bias=nw["e"][:, 5, c:c + 1], scale=nw["e"][:, 4, c:c + 1]).then_inc(xn_done, 1)
                if "O" in at:
                    j, p, r = at["O"]
                    layer_norm_act(act, "r", j)
                    act.wait_ge(newton["r"], j * 4 + 4)
                    wait(act, scattered[p], r * 2 * NT * 16)
                    for c in range(NT):
                        act.activation(rows[p][:, c, 0:D], x1[p][:, c, :], ACT.Identity,
                                       bias=nw["r"][:, 5, c:c + 1], scale=nw["r"][:, 4, c:c + 1]).then_inc(rows_done, 1)

            run_steps(act, step)

            def gather_T(i, p):
                act.wait_ge(gT_mm, i + 1)
                wait(act, h_mm, (i - 1) * FC)
                act.activation(xgT[p][:], gT_ps[p][:, 0:T], ACT.Copy).then_inc(gT_sb, 1)

            def gelu(i, p):
                bias = we[p]
                for f in range(FC):
                    if f % 2 == 0:
                        act.wait_ge(h_mm, i * FC + f + 2)
                    if f == 0:
                        wait(act, y_mm, i - 1)
                    act.activation(hid[p][:, f, :], h_ps(p, f), ACT.Gelu_apprx_tanh,
                                   bias=bias[:, 2 * FF + f:2 * FF + f + 1]).then_inc(h_done, 1)

            gather_T(0, 0)
            for i in range(2):
                gather_T(i + 1, 1 - i)
                gelu(i, i)
            with act.Fori(1, MOE_TILES // 2) as t:
                for p in range(2):
                    gather_T(2 * t + p + 1, 1 - p)
                    gelu(2 * t + p, p)
            gelu(MOE_TILES - 1, 0)

            def last(j, p, r):
                act.wait_ge(y_in[p], r * 32 + 32)
                act.wait_ge(pc_done, j + 1)
                wait(act, ys_done, (j - 1) * NT)
                for c in range(NT):
                    act.activation(yp[p][:, c, :], y0[p][:, c, :], ACT.Copy, scale=pc[p][:, 2 * c:2 * c + 1]
                                   ).then_inc(yp_done, 1)
                layer_norm_act(act, "c", j)
                act.wait_ge(newton["c"], j * 4 + 4)
                wait(act, fin_done, j - 1)
                for c in range(NT):
                    act.activation(yn[p][:, c, :], ys[p][:, c, :], ACT.Identity,
                                   bias=nw["c"][:, 5, c:c + 1], scale=nw["c"][:, 4, c:c + 1]).then_inc(yn_done, 1)

            for j in range(2):
                last(j, j, 0)
            with act.Fori(1, B // 2) as t:
                for p in range(2):
                    last(2 * t + p, p, t)

        @block.tensor
        def _(pe):
            pe.wait_ge(consts_in, n_const)
            pe.matmul(st_ps[0:1, 0:D], b_v[:], w_o[:], start=True, stop=False)
            pe.wait_ge(init, 5)
            pe.matmul(st_ps[0:1, 0:D], ones_row[0:1, 0:1], b_o[:], start=False, stop=True).then_inc(bias_mm, 1)
            pe.wait_ge(init_a, 1)

            def prefix(at, c):
                if "M" not in at:
                    return
                j, p, r = at["M"]
                b = c % 2
                qt, kt = qk[p][:, c, 0:D], qk[p][:, c, D:2 * D]
                if c == 0:
                    pe.wait_ge(v_sb, j + 1)
                    pe.wait_ge(qk_sb, j * 2 + 2)
                wait(pe, m_prod, (j * NT + c) * 3)
                wait(pe, m_tot, (j * (NT - 1) + max(c - 1, 0)))
                pe.matmul(k1_ps, tri_s[:], kt, start=True, stop=True).then_inc(k1_mm, 1)
                if c < NT - 1:
                    wait(pe, state_sb, j * (NT - 1) + c)
                    pe.matmul(st_ps[:, 0:HV], kt, vx[p][:, c, :], start=(c == 0), stop=True,
                              skip_group_check=True).then_inc(state_mm, 1)
                if c > 0:
                    if c == NT - 1:
                        wait(pe, state_sb, j * (NT - 1) + c)
                    pe.matmul(inter_ps, qkT[p][:, c * P:(c + 1) * P], state[(c - 1) % 2][:], start=True, stop=True)
                pe.wait_ge(outer, j * NT + c + 1)
                for k in range(2):
                    m = pe.matmul(kv_ps[k][:], tri_s[:], kv[b][:, k * 512:(k + 1) * 512], start=True, stop=True)
                m.then_inc(cum, 1)

            def step(at):
                F, O, R = at.get("F"), at.get("O"), at.get("R")
                prefix(at, 0)
                if F:
                    j, p, r = F
                    pe.wait_ge(xn_done, j * NT + NT)
                    wait(pe, v_sb, j)
                    wait(pe, slots, (j - OFFSETS["R"] + OFFSETS["F"]) * 7)
                    for c in range(NT):
                        m = pe.transpose(xv_ps[:, c * P:(c + 1) * P], xn[p][:, c, :], idn[:])
                    m.then_inc(xnT_mm, 1)
                if R:
                    j, p, r = R
                    pe.wait_ge(rows_done, j * NT + NT)
                    wait(pe, an_done, (j + 1) * NT)
                    for c in range(NT):
                        m = pe.transpose(out_ps[:, c * P:(c + 1) * P], rows[p][:, c, 0:D], idn[:])
                    m.then_inc(x2T_mm, 1)
                if F:
                    j, p, r = F
                    pe.wait_ge(xnT_sb, j + 1)
                    wait(pe, qk_sb, j * 2)
                    for k in range(2):
                        m = pe.matmul(qk_ps[:, k * S:(k + 1) * S], w_qkv[:, k * D:(k + 1) * D], xnT[:],
                                      start=True, stop=True)
                    m.then_inc(qk_mm, 1)
                    for c in range(NT):
                        m = pe.matmul(xv_ps[:, c * D:(c + 1) * D], xnT[:, c * P:(c + 1) * P], w_qkv[:, 2 * D:3 * D],
                                      start=True, stop=True)
                    m.then_inc(v_mm, 1)
                if R:
                    j, p, r = R
                    pe.wait_ge(x2T_sb, j + 1)
                    for c in range(NT):
                        m = pe.matmul(logit_ps[:, c, :], xn2T[:, c * P:(c + 1) * P], w_gate[:], start=True, stop=True)
                    m.then_inc(logit_mm, 1)
                prefix(at, 1)
                if O:
                    j, p, r = O
                    pe.wait_ge(o_done, j * NT + NT)
                    wait(pe, an_done, j * NT)
                    if R:
                        pe.wait_ge(route, R[0] * 13 + 1)
                    for c in range(NT):
                        m = pe.transpose(out_ps[:, c * P:(c + 1) * P], o[p][:, c, :], idn[:])
                    m.then_inc(oT_mm, 1)
                prefix(at, 2)
                if O:
                    j, p, r = O
                    pe.wait_ge(oT_sb, j + 1)
                    for c in range(NT):
                        pe.matmul(out_ps[:, c * D:(c + 1) * D], ones_row[:], attn_bias[:], start=True, stop=False)
                        m = pe.matmul(out_ps[:, c * D:(c + 1) * D], oT[:, c * P:(c + 1) * P], w_o[:],
                                      start=False, stop=True)
                    m.then_inc(a_mm, 1)
                if F:
                    j, p, r = F
                    pe.wait_ge(soft_sum, j + 1)
                    for c in range(NT):
                        for k in range(2):
                            m = pe.transpose(qk_ps[:, (2 * c + k) * P:(2 * c + k + 1) * P],
                                             qkT[p][:, k * S + c * P:k * S + (c + 1) * P], idn[:])
                    m.then_inc(qkt_mm, 1)
                prefix(at, 3)
                if R:
                    j, p, r = R
                    pe.wait_ge(route, j * 13 + 12)
                    if F:
                        pe.wait_ge(v_sb, F[0] + 1)
                    wait(pe, slots, j * 7)
                    for c in range(NT):
                        pe.matmul(rank_ps[:, c, :], tri_b[:], hot_b[:, c, :], start=True, stop=(c == 0))
                        for b in range(c):
                            pe.matmul(rank_ps[:, c, :], ones_b[:], hot_b[:, b, :], start=False, stop=(b == c - 1))
                    for c in range(NT):
                        m = pe.matmul(count_ps, ones_b[:], hot_b[:, c, :], start=(c == 0), stop=(c == NT - 1))
                    m.then_inc(rank_mm, 1)

            run_steps(pe, step)

            def gather_T(i, p, r):
                pe.wait_ge(xg_in[p], r * 16 + 16)
                wait(pe, gT_sb, i - 1)
                for k in range(2):
                    m = pe.transpose(gT_ps[p][:, k * P:(k + 1) * P], xg[p][:, k, 0:D], idn[:])
                m.then_inc(gT_mm, 1)

            def up(i, p):
                pe.wait_ge(gT_sb, i + 1)
                pe.wait_ge(we_done, i + 1)
                wait(pe, h_done, (i - 1) * FC)
                for f in range(FC):
                    pe.matmul(h_ps(p, f), we[p][:, f * P:(f + 1) * P], xgT[p][:], start=True, stop=True).then_inc(h_mm, 1)

            def down(i, p):
                pe.wait_ge(h_done, i * FC + FC)
                wait(pe, y_done, i - 1)
                for k in range(2):
                    for f in range(FC):
                        m = pe.matmul(y_ps[p][:, k * D:(k + 1) * D], hid[p][:, f, k * P:(k + 1) * P],
                                      we[p][:, FF + f * D:FF + (f + 1) * D], start=(f == 0), stop=(f == FC - 1))
                m.then_inc(y_mm, 1)

            pe.wait_ge(an_done, B * NT)
            pe.wait_ge(x2T_sb, B)
            pe.wait_ge(m_tot, B * (NT - 1))
            pe.wait_ge(slots, B * 7)
            pe.wait_ge(m_prod, B * NT * 3)
            gather_T(0, 0, 0)
            gather_T(1, 1, 0)
            up(0, 0)
            gather_T(2, 0, 1)
            up(1, 1)
            down(0, 0)
            with pe.Fori(1, MOE_TILES // 2) as t:
                for p in range(2):
                    gather_T(2 * t + p + 1, 1 - p, t + p)
                    up(2 * t + p, p)
                    down(2 * t + p - 1, 1 - p)
            up(MOE_TILES - 1, 0)
            down(MOE_TILES - 2, 1)
            down(MOE_TILES - 1, 0)

        @block.vector
        def _(v):
            v.memset(eps_t[:], EPS).then_inc(init, 1)
            v.memset(ones_row[:], 1.0).then_inc(init, 1)
            v.memset(ones_b[:], 1.0).then_inc(init, 1)
            for k in range(2):
                v.memset(vx[k][:].rearrange("p c (h w) -> p (c h) w", w=DEN)[:, :, DH:DEN], 1.0)
            v.memset(rows[0][:, :, D:RW], 0.0)
            v.memset(rows[1][:, :, D:RW], 0.0)
            v.wait_ge(consts_in, n_const)
            v.tensor_copy(tri_b[:], tri_strict[:]).then_inc(init, 1)
            v.tensor_copy(base[:], ecap).then_inc(init, 1)
            v.tensor_copy(token[:], tok0).then_inc(init, 1)
            v.wait_ge(init, 6)

            def head(at, c):
                if "M" not in at:
                    return
                j, p, r = at["M"]
                b = c % 2
                q = qk[p][:, c, 0:D].rearrange("p (h d) -> p h d", h=H)
                if c < NT - 1:
                    v.wait_ge(state_mm, j * (NT - 1) + c + 1)
                    wait(v, cum, j * NT + c)
                    v.tensor_tensor(state[c % 2][:], st_ps[:, 0:HV], head_mask[:], ALU.mult).then_inc(state_sb, 1)
                v.wait_ge(cum, j * NT + c + 1)
                v.tensor_tensor(prod[b][:, :, :, DH], k1_ps.rearrange("p (h d) -> p h d", h=H), q, ALU.mult
                                ).then_inc(m_prod, 1)
                for k in range(2):
                    hs = slice(k * 8, k * 8 + 8)
                    v.tensor_tensor(prod[b][:, hs, :, 0:DH],
                                    kv_ps[k][:].rearrange("p (h d e) -> p h d e", h=8, d=DH),
                                    q[:, hs, :, None].broadcast_to((P, 8, DH, DH)), ALU.mult).then_inc(m_prod, 1)
                v.wait_ge(m_prod, (j * NT + c) * 3 + 3)
                v.tensor_reduce(num[b][:], prod[b][:].rearrange("p h d e -> p h e d"), AX, ALU.add).then_inc(m_red, 1)
                v.wait_ge(m_red, j * NT + c + 1)
                total = num[b]
                if c > 0:
                    total = tot[b]
                    v.tensor_tensor(tot[b][:], num[b][:], inter_ps.rearrange("p (h w) -> p h w", h=H), ALU.add
                                    ).then_inc(m_tot, 1)
                    v.wait_ge(m_tot, j * (NT - 1) + c)
                v.reciprocal(rden[b][:], total[:, :, DH]).then_inc(m_rden, 1)
                v.wait_ge(m_rden, j * NT + c + 1)
                if c == 0:
                    wait(v, oT_mm, j - 1)
                v.tensor_tensor(o[p][:, c, :].rearrange("p (h e) -> p h e", h=H), total[:, :, 0:DH],
                                rden[b][:, :, None].broadcast_to((P, H, DH)), ALU.mult).then_inc(o_done, 1)

            def step(at):
                F, O, R, E_ = at.get("F"), at.get("O"), at.get("R"), at.get("E")
                head(at, 0)
                if R:
                    j, p, r = R
                    n0 = j * 13
                    v.wait_ge(logit_mm, j + 1)
                    v.tensor_copy(logit[:], logit_ps).then_inc(route, 1)
                    hold(v, (route, n0 + 1))
                    for c in range(NT):
                        v.max(top[:, c, :], logit[:, c, :]).then_inc(route, 1)
                    hold(v, (route, n0 + 5), (etop_done, j))
                    for c in range(NT):
                        m = v.max_index(topi[:, c, :], top[:, c, :], logit[:, c, :])
                        if c < NT - 1:
                            m.then_inc(route, 1)
                        else:
                            m.then_inc(meta, 1)
                    v.wait_ge(route, n0 + 5)
                    v.tensor_tensor(dtop[:], top[:], top[:, :, 0:1].broadcast_to((P, NT, E)), ALU.subtract
                                    ).then_inc(route, 1)
                    v.wait_ge(meta, j * 4 + 1)
                    v.tensor_copy(topf[:], topi[:, :, 0:2]).then_inc(route, 1)
                head(at, 1)
                if R:
                    j, p, r = R
                    n0 = j * 13
                    v.wait_ge(route, n0 + 10)
                    v.tensor_tensor(hot[:], iota8[:, None, None, :].broadcast_to((P, NT, 2, E)),
                                    topf[:, :, :, None].broadcast_to((P, NT, 2, E)), ALU.is_equal).then_inc(route, 1)
                    wait(v, scattered[p], r * 2 * NT * 16)
                    v.tensor_copy(rows[p][:, :, D + 1], topf[:, :, 0]).then_inc(meta, 1)
                    v.tensor_copy(rows[p][:, :, D], token[:]).then_inc(meta, 1)
                    v.wait_ge(route, n0 + 11)
                    wait(v, rank_mm, j)
                    v.tensor_tensor(hot_b[:], hot[:, :, 0, :], hot[:, :, 1, :], ALU.add).then_inc(route, 1)
                    v.wait_ge(meta, j * 4 + 3)
                    v.tensor_scalar(token[:], token[:], float(S), None, ALU.add).then_inc(meta, 1)
                if F:
                    j, p, r = F
                    v.wait_ge(soft_a, j * 6 + 6)
                    wait(v, qkt_mm, j - 1)
                    wait(v, cum, (j - 1) * NT)
                    v.tensor_tensor(qkT[p][:], f_ln[:], f_relu[:], ALU.add).then_inc(soft_sum, 1)
                head(at, 2)
                if O:
                    j, p, r = O

                    def waits():
                        v.wait_ge(a_mm, j + 1)
                    layer_norm_stats(v, "a", j, lambda c: out_ps[:, c * D:(c + 1) * D], None, waits)
                if R:
                    j, p, r = R
                    n0 = j * 13
                    first = tile_of(v, j)
                    v.wait_ge(etop_done, j + 1)
                    v.tensor_reduce(zsum[:], etop[:], AX, ALU.add).then_inc(slots, 1)
                    v.wait_ge(slots, j * 7 + 1)
                    v.reciprocal(rz[:], zsum[:]).then_inc(slots, 1)
                    v.wait_ge(slots, j * 7 + 2)
                    v.tensor_tensor(prob_all[:, bass.ds(first, NT), :],
                                    etop[:, :, 0:2], rz[:, :, None].broadcast_to((P, NT, 2)), ALU.mult
                                    ).then_inc(route, 1)
                head(at, 3)
                if O:
                    layer_norm_newton(v, "a", O[0])
                if E_:
                    j, p, r = E_

                    def waits():
                        v.wait_ge(xe_in[p], r * 16 + 16)
                    layer_norm_stats(v, "e", j, lambda c: xe[p][:, c, :], None, waits)
                    layer_norm_newton(v, "e", j)
                if O:
                    j, p, r = O

                    def waits():
                        v.wait_ge(x1_done, j + 1)
                    layer_norm_stats(v, "r", j, lambda c: x1[p][:, c, :], None, waits)
                if R:
                    j, p, r = R
                    n0 = j * 7
                    v.wait_ge(rank_mm, j + 1)
                    v.tensor_tensor(pos[:], rank_ps, base[:, None, :].broadcast_to((P, NT, E)), ALU.add
                                    ).then_inc(slots, 1)
                    v.wait_ge(slots, n0 + 3)
                    v.tensor_tensor(base[:], base[:], count_ps, ALU.add).then_inc(slots, 1)
                    v.tensor_tensor(psel[:], hot[:], pos[:, :, None, :].broadcast_to((P, NT, 2, E)), ALU.mult
                                    ).then_inc(slots, 1)
                    v.wait_ge(slots, n0 + 5)
                    v.tensor_reduce(slotf[:].rearrange("p (c k) -> p c k", k=2), psel[:], AX, ALU.add
                                    ).then_inc(slots, 1)
                    v.wait_ge(slots, n0 + 6)
                    wait(v, scattered[p], r * 2 * NT * 16)
                    v.tensor_copy(slot[p][:], slotf[:]).then_inc(slots, 1)
                if O:
                    layer_norm_newton(v, "r", O[0])

            run_steps(v, step)

            tn = [0]

            def t_op(ins):
                tn[0] += 1
                ins.then_inc(table, 1)
                v.wait_ge(table, tn[0])

            t_op(v.tensor_tensor(cnt[:], base[:], ecap, ALU.subtract))
            t_op(v.tensor_tensor(cmp32[:], cnt[:, :, None].broadcast_to((P, E, 32)),
                                 m256[:, None, :].broadcast_to((P, E, 32)), ALU.is_gt))
            t_op(v.tensor_reduce(ntile[:], cmp32[:], AX, ALU.add))
            t_op(v.tensor_tensor(trie[:], lower, ntile[:, None, :].broadcast_to((P, E, E)), ALU.mult))
            t_op(v.tensor_reduce(tend[:], trie[:], AX, ALU.add))
            t_op(v.tensor_tensor(ge[:], tnum[:, :, None].broadcast_to((P, MOE_TILES, E)),
                                 tend[:, None, :].broadcast_to((P, MOE_TILES, E)), ALU.is_ge))
            t_op(v.tensor_reduce(ex_of[:], ge[:], AX, ALU.add))
            t_op(v.tensor_tensor(gen[:], ge[:], ntile[:, None, :].broadcast_to((P, MOE_TILES, E)), ALU.mult))
            t_op(v.tensor_reduce(t_start[:], gen[:], AX, ALU.add))
            t_op(v.tensor_tensor(row_of[:], tnum, t_start[:], ALU.subtract))
            t_op(v.tensor_scalar(row_b[:], row_of[:], float(T), None, ALU.mult))
            t_op(v.scalar_tensor_tensor(row_of[:], ex_of[:], float(CAP), row_b[:], ALU.mult, ALU.add))
            t_op(v.tensor_scalar(row_b[:], row_of[:], float(E * CAP), None, ALU.min))
            t_op(v.tensor_copy(row_i[:], row_b[:]))
            t_op(v.tensor_scalar(ex_min[:], ex_of[:], float(E - 1), None, ALU.min))
            t_op(v.tensor_copy(ex_i[:], ex_min[:]))
            while tn[0] < 20:
                t_op(v.tensor_copy(end_i[:], base[:]))
            v.wait_ge(w_in, 16)

            def expert(i, p):
                e = v.value_load(ex_i[0:1, bass.ds(i, 1)], min_val=0, max_val=E - 1)
                hold(v, (y_done, i - 1), (dest_done, i - 1))
                v.tensor_copy(we[p][:], W[:, bass.ds(e, 1), :].rearrange("p a w -> p (a w)")).then_inc(we_done, 1)

            def where(i, p, r):
                v.wait_ge(we_done, i + 1)
                v.wait_ge(xg_in[p], r * 16 + 16)
                v.tensor_scalar(second[p][:], xg[p][:, :, D + 1], we[p][:, WW - 2:WW - 1], float(N),
                                ALU.not_equal, ALU.mult).then_inc(dest_a, 1)
                v.wait_ge(dest_a, i + 1)
                wait(v, y_sent[p], r * 32)
                v.tensor_tensor(dest[p][:], second[p][:], xg[p][:, :, D], ALU.add).then_inc(dest_done, 1)

            def finish(i, p, r):
                v.wait_ge(y_mm, i + 1)
                wait(v, y_sent[p], r * 32)
                v.tensor_tensor(yv[p][:], y_ps[p][:, 0:T].rearrange("p (k d) -> p k d", k=2),
                                we[p][:, None, 2 * FF + FC:2 * FF + FC + D].broadcast_to((P, 2, D)), ALU.add
                                ).then_inc(y_done, 1)

            expert(0, 0)
            expert(1, 1)
            where(0, 0, 0)
            where(1, 1, 0)
            finish(0, 0, 0)
            expert(2, 0)
            where(2, 0, 1)
            with v.Fori(1, MOE_TILES // 2) as t:
                finish(2 * t - 1, 1, t - 1)
                expert(2 * t + 1, 1)
                where(2 * t + 1, 1, t)
                finish(2 * t, 0, t)
                expert(2 * t + 2, 0)
                where(2 * t + 2, 0, t + 1)
            finish(MOE_TILES - 2, 1, MOE_TILES // 2 - 1)
            finish(MOE_TILES - 1, 0, MOE_TILES // 2)

            def last(j, p, r):
                first = tile_of(v, j)
                hold(v, (ys_done, (j - 1) * NT), (yp_done, (j - 1) * NT))
                v.tensor_copy(pc[p][:], prob_all[:, bass.ds(first, NT), :].rearrange("p c k -> p (c k)")
                              ).then_inc(pc_done, 1)
                v.wait_ge(pc_done, j + 1)
                wait(v, yn_done, (j - 1) * NT)
                for c in range(NT):
                    v.wait_ge(yp_done, j * NT + c + 1)
                    v.scalar_tensor_tensor(ys[p][:, c, :], y1[p][:, c, :], pc[p][:, 2 * c + 1:2 * c + 2],
                                           yp[p][:, c, :], ALU.mult, ALU.add).then_inc(ys_done, 1)

                def waits():
                    v.wait_ge(ys_done, j * NT + NT)
                layer_norm_stats(v, "c", j, lambda c: ys[p][:, c, :], None, waits)
                layer_norm_newton(v, "c", j)

            for p in range(2):
                v.wait_ge(x1_kept[p], B // 2 * 16)
            for j in range(2):
                last(j, j, 0)
            with v.Fori(1, B // 2) as t:
                for p in range(2):
                    last(2 * t + p, p, t)

        @block.gpsimd
        def _(gp):
            gp.wait_ge(init, 6)

            def step(at):
                M, O, S_ = at.get("M"), at.get("O"), at.get("S")
                for c in range(NT):
                    if M:
                        j, p, r = M
                        if c == 0:
                            gp.wait_ge(qk_sb, j * 2 + 2)
                            gp.wait_ge(v_sb, j + 1)
                        wait(gp, cum, j * NT + c - 1)
                        gp.tensor_tensor(
                            kv[c % 2][:].rearrange("p (h d e) -> p h d e", h=H, d=DH),
                            qk[p][:, c, D:2 * D].rearrange("p (h d) -> p h d", h=H)[:, :, :, None]
                            .broadcast_to((P, H, DH, DH)),
                            vx[p][:, c, :].rearrange("p (h w) -> p h w", w=DEN)[:, :, None, 0:DH]
                            .broadcast_to((P, H, DH, DH)), ALU.mult).then_inc(outer, 1)
                    if S_:
                        j, p, r = S_
                        if c == 0:
                            hold(gp, (slots, j * 7 + 7), (meta, j * 4 + 4), (rows_done, j * NT + NT))
                        for k in range(2):
                            gp.indirect_dma_start(
                                out=bucket, out_offset=bass.IndirectOffsetOnAxis(
                                    ap=slot[p][:, 2 * c + k:2 * c + k + 1], axis=0),
                                in_=rows[p][:, c, :], in_offset=None).then_inc(scattered[p], 16)
                    if O and c == NT - 1:
                        j, p, r = O
                        gp.wait_ge(an_done, j * NT + NT)
                        gp.wait_ge(xr_in[p], r * 16 + 16)
                        wait(gp, x1_kept[p], r * 16)
                        wait(gp, rows_done, (j - 1) * NT)
                        gp.tensor_tensor(x1[p][:], an[:], xr[p][:], ALU.add).then_inc(x1_done, 1)

            run_steps(gp, step)

            def send(i, p, r):
                hold(gp, (y_done, i + 1), (dest_done, i + 1))
                for k in range(2):
                    gp.indirect_dma_start(
                        out=ychoice, out_offset=bass.IndirectOffsetOnAxis(ap=dest[p][:, k:k + 1], axis=0),
                        in_=yv[p][:, k, :], in_offset=None, bounds_check=2 * N - 1, oob_is_err=False
                    ).then_inc(y_sent[p], 16)

            for i in range(2):
                send(i, i, 0)
            with gp.Fori(1, MOE_TILES // 2) as t:
                for p in range(2):
                    send(2 * t + p, p, t)
            send(MOE_TILES - 1, 0, MOE_TILES // 2)

            for p in range(2):
                gp.wait_ge(x1_kept[p], B // 2 * 16)

            def last(j, p, r):
                first = tile_of(gp, j)
                hold(gp, (yn_done, j * NT + NT), (stored[p], r * 16))
                gp.tensor_tensor(fin[p], yn[p][:], x1_all[:, bass.ds(first, NT), :], ALU.add).then_inc(fin_done, 1)

            for j in range(2):
                last(j, j, 0)
            with gp.Fori(1, B // 2) as t:
                for p in range(2):
                    last(2 * t + p, p, t)


def kernel(**inputs):
    import numpy as np
    import concourse.bacc as bacc
    from concourse.bass_utils import run_bass_kernel_spmd as run

    a = {k.split("_", 1)[1]: np.asarray(v) for k, v in inputs.items()}
    f = np.float32
    w1 = a["ffn_w1"].transpose(2, 1, 0)
    w2 = a["ffn_w2"].reshape(D, E, FC, P).transpose(3, 1, 2, 0).reshape(P, E, FC * D)
    b1 = a["ffn_b1"].reshape(E, FC, P).transpose(2, 0, 1)
    b2 = np.broadcast_to(a["ffn_b2"][None], (P, E, D))
    number = np.zeros((P, E, 2), f)
    number[:, :, 0] = np.arange(E)
    pad = np.zeros((T, RW), f)
    pad[:, D] = N + np.arange(T)
    pad[:, D + 1] = -1
    consts = np.zeros((P, 188), f)
    consts[:, 0:E] = np.arange(E)
    consts[:, E:2 * E] = np.arange(E) * CAP
    consts[:, 16:48] = np.arange(32) * T
    consts[:, 48:112] = np.tril(np.ones((E, E))).reshape(-1)
    consts[:, 112:112 + MOE_TILES] = np.arange(MOE_TILES)
    consts[:, 183:187] = np.arange(P)[:, None] + P * np.arange(NT)[None]
    heads = np.arange(P) // DH
    mask = (heads[:, None] == np.arange(HV)[None] // DEN).astype(f)
    arrays = {
        "x": a["attn_x"],
        "wqkvT": np.concatenate([a["attn_Wq"].T, a["attn_Wk"].T, a["attn_Wv"].T], 1),
        "woT": a["attn_Wo"].T, "gateT": a["ffn_gate_w"].T,
        "bqk": np.stack([a["attn_bq"], a["attn_bk"]], 1), "bv": a["attn_bv"][:, None], "bo": a["attn_bo"][None],
        "wexp": np.concatenate([w1, w2, b1, b2, number], 2),
        "ident": np.eye(P, dtype=f), "tri": np.triu(np.ones((P, P), f)), "stri": np.triu(np.ones((P, P), f), 1),
        "mask": mask, "consts": consts, "pad": pad.reshape(P, 2 * RW),
    }
    arrays = {f"in_{k}": np.ascontiguousarray(v) for k, v in arrays.items()}
    nc = bacc.Bacc("TRN2", target_bir_lowering=False, num_devices=1)
    args = [nc.dram_tensor(k, v.shape, mybir.dt.from_np(v.dtype), kind="ExternalInput").ap() for k, v in arrays.items()]
    out = nc.dram_tensor("out_0", (B, S, D), F32, kind="ExternalOutput").ap()
    build(nc, *args, out)
    r = run(nc, [arrays], core_ids=[0])
    return r.results[0]["out_0"]
```

```python
from contextlib import ExitStack

import concourse.bass as bass
from concourse import mybir

F32 = mybir.dt.float32
BF16 = mybir.dt.bfloat16
I32 = mybir.dt.int32
U32 = mybir.dt.uint32
ALU = mybir.AluOpType
ACT = mybir.ActivationFunctionType
AX = mybir.AxisListType.X

P = 128
B, S, D = 16, 512, 128
H, DH = 16, 8
NT = S // P
N = B * S
E, FF = 8, 512
FC = FF // P
DEN = DH + 1
HV = H * DEN
T = 256
CAP = N + T
RING = 4
MOE_TILES = (2 * N + E * (T - 1)) // T
RW = 132
WW = 2 * FF + FC + D + 2
EPS = 1e-5
OFFSETS = dict(E=0, F=1, M=2, O=3, Q=4, W=4, R=5, S=6)
STEPS = B + 6
TABLE_OPS = 17
PRODS = (0, 3, 7, 11, 15)

PARAMS = dict(ident=P, w_qkv=3 * D, b_qk=2, w_o=D, w_gate=E, b_v=1, b_o=D, tri=P, tri_strict=P, mask=HV, con=188)


def wait(eng, sem, value):
    if isinstance(value, int) and value <= 0:
        return
    eng.wait_ge(sem, value)


def build(nc, x, params, wexp, pad, out):
    bucket = nc.dram_tensor("bucket", (E * CAP + T, RW), F32, kind="Internal").ap()
    ychoice = nc.dram_tensor("ychoice", (2 * N, D), F32, kind="Internal").ap()
    x_v = x.rearrange("b (c p) d -> p (b c) d", p=P)
    out_v = out.rearrange("b (c p) d -> p (b c) d", p=P)
    y_v = ychoice.rearrange("(k t p) d -> k p t d", k=2, p=P)

    with ExitStack() as ctx:
        def sb(name, shape, dt=F32):
            return ctx.enter_context(nc.sbuf_tensor(name, shape, dt))

        def ps(name, shape, dt=F32):
            return ctx.enter_context(nc.psum_tensor(name, shape, dt))

        def sem(name):
            return ctx.enter_context(nc.semaphore(name))

        def pair(name):
            return [sem(f"{name}{k}") for k in range(2)]

        par = sb("par", [P, sum(PARAMS.values())])
        at_col, part = 0, {}
        for name, width in PARAMS.items():
            part[name] = par[:, at_col:at_col + width]
            at_col += width
        w_qkv, w_o, w_gate, b_qk, b_v, idn, tri_s, tri_strict, head_mask, con = (
            part[k] for k in ("w_qkv", "w_o", "w_gate", "b_qk", "b_v", "ident", "tri", "tri_strict", "mask", "con"))
        b_o = part["b_o"][0:1, :]
        attn_bias = sb("attn_bias", [1, D])
        tri_b = sb("tri_b", [P, P], BF16)
        ones_b = sb("ones_b", [P, P], BF16)
        ones_row = sb("ones_row", [1, P])
        eps_t = sb("eps_t", [P, 1])
        W = sb("W", [P, E, WW])
        pad_rows = sb("pad_rows", [P, 2 * RW])
        xe = [sb(f"xe{k}", [P, NT, D]) for k in range(2)]
        xr = [sb(f"xr{k}", [P, NT, D]) for k in range(2)]
        xn = [sb(f"xn{k}", [P, NT, D]) for k in range(2)]
        xnT = sb("xnT", [P, S])
        f_abs = sb("f_abs", [P, 2 * S])
        f_exp = sb("f_exp", [P, 2 * S])
        f_ln = sb("f_ln", [P, 2 * S])
        f_relu = sb("f_relu", [P, 2 * S])
        qkT = [sb(f"qkT{k}", [P, 2 * S]) for k in range(2)]
        qk = [sb(f"qk{k}", [P, NT, 2 * D]) for k in range(2)]
        vx = [sb(f"vx{k}", [P, NT, HV]) for k in range(2)]
        kv = [sb(f"kv{k}", [P, H * DH * DH]) for k in range(2)]
        prod = [sb(f"prod{k}", [P, H, DEN, DEN]) for k in range(2)]
        num = sb("num", [P, NT, H, DEN])
        rden = sb("rden", [P, NT, H])
        state = [sb(f"state{k}", [P, HV]) for k in range(2)]
        o = [sb(f"o{k}", [P, NT, D]) for k in range(2)]
        oT = sb("oT", [P, S])
        an = sb("an", [P, NT, D])
        x1 = [sb(f"x1{k}", [P, NT, D]) for k in range(2)]
        rows = [sb(f"rows{k}", [P, NT, RW]) for k in range(2)]
        xn2T = sb("xn2T", [P, S])
        logit = sb("logit", [P, NT, E])
        top = sb("top", [P, NT, E])
        topi = sb("topi", [P, NT, E], U32)
        topf = sb("topf", [P, NT, 2])
        dtop = sb("dtop", [P, NT, E])
        etop = sb("etop", [P, NT, E])
        zsum = sb("zsum", [P, NT])
        rz = sb("rz", [P, NT])
        hot = sb("hot", [P, NT, 2, E])
        hot_b = sb("hot_b", [P, NT, E], BF16)
        base = sb("base", [P, E])
        pos = sb("pos", [P, NT, E])
        psel = sb("psel", [P, NT, 2, E])
        slotf = sb("slotf", [P, NT * 2])
        slot = [sb(f"slot{k}", [P, NT * 2], I32) for k in range(2)]
        token = sb("token", [P, NT])
        st = {k: sb(f"st_{k}", [P, NT, 6]) for k in "earc"}
        mv = {k: sb(f"mv_{k}", [P, NT, 2]) for k in "ec"}
        mv["ar"] = sb("mv_ar", [P, 2 * NT, 2])
        mv["a"], mv["r"] = mv["ar"][:, 0:NT, :], mv["ar"][:, NT:2 * NT, :]
        nw = {k: sb(f"nw_{k}", [P, 6, len(k) * NT]) for k in ("e", "ar", "c")}
        x1_all = sb("x1_all", [P, B * NT, D])
        prob_all = sb("prob_all", [P, B * NT, 2])
        cnt = sb("cnt", [P, E])
        cmp32 = sb("cmp32", [P, E, 32])
        ntile = sb("ntile", [P, E])
        trie = sb("trie", [P, E, E])
        tend = sb("tend", [P, E])
        ge = sb("ge", [P, MOE_TILES, E])
        gen = sb("gen", [P, MOE_TILES, E])
        ex_of = sb("ex_of", [P, MOE_TILES])
        t_start = sb("t_start", [P, MOE_TILES])
        row_of = sb("row_of", [P, MOE_TILES])
        row_b = sb("row_b", [P, MOE_TILES])
        ex_min = sb("ex_min", [P, MOE_TILES])
        row_i = sb("row_i", [P, MOE_TILES], I32)
        ex_i = sb("ex_i", [P, MOE_TILES], I32)
        end_i = sb("end_i", [P, E], I32)
        xg = [sb(f"xg{k}", [P, 2, RW]) for k in range(RING)]
        we = [sb(f"we{k}", [P, WW]) for k in range(RING)]
        xgT = [xnT[:, k * T:(k + 1) * T] for k in range(2)]
        hid = [f[:].rearrange("p (f t) -> p f t", f=FC) for f in (f_exp, f_ln)]
        yv = [f_abs[:, k * T:(k + 1) * T].rearrange("p (k d) -> p k d", k=2) for k in range(RING)]
        second = [sb(f"second{k}", [P, 2]) for k in range(RING)]
        dest = [sb(f"dest{k}", [P, 2], I32) for k in range(RING)]
        y0, y1 = ([*t, *(q[:, k * S:(k + 1) * S].rearrange("p (c d) -> p c d", c=NT) for k in range(2))]
                  for t, q in ((xe, qkT[0]), (xr, qkT[1])))
        ys = [*x1, *(f_relu[:, k * S:(k + 1) * S].rearrange("p (c d) -> p c d", c=NT) for k in range(2))]
        yp, yn, fin = xn, o, [rows[k][:, :, 0:D] for k in range(2)]
        pc = [sb(f"pc{k}", [P, NT * 2]) for k in range(2)]

        kv_ps = [ps(f"kv_ps{k}", [P, 512]) for k in range(2)]
        small = ps("small", [P, 512])
        st_ps = ps("st_ps", [P, 512])
        qk_ps = ps("qk_ps", [P, 1024])
        xv_ps = ps("xv_ps", [P, 512])
        out_ps = ps("out_ps", [P, 512])
        k1_ps = small[:, 0:D]
        inter_ps = small[:, D:D + HV]
        logit_ps, rank_ps = (st_ps[:, a:a + NT * E].rearrange("p (c e) -> p c e", c=NT) for a in (HV, HV + NT * E))
        count_ps = st_ps[:, HV + 2 * NT * E:HV + 2 * NT * E + E]
        gT_ps, y_ps = (xv_ps, st_ps), (out_ps, small)

        iota8 = con[:, 0:E]
        ecap = con[:, E:2 * E]
        m256 = con[:, 16:48]
        lower = con[:, 48:48 + E * E].rearrange("p (a b) -> p a b", a=E)
        tnum = con[:, 112:112 + MOE_TILES]
        tok0 = con[:, 183:183 + NT]

        consts_in, w_in = sem("consts_in"), sem("w_in")
        init, init_a = sem("init"), sem("init_a")
        bias_mm, bias_row = sem("bias_mm"), sem("bias_row")
        xe_in, xr_in = pair("xe_in"), pair("xr_in")
        stat = {k: sem(f"stat_{k}") for k in "earc"}
        lnexp = {k: sem(f"lnexp_{k}") for k in ("e", "ar", "c")}
        newton = {k: sem(f"newton_{k}") for k in ("e", "ar", "c")}
        xn_done = sem("xn_done")
        xnT_mm, xnT_sb = sem("xnT_mm"), sem("xnT_sb")
        qk_mm, v_mm, v_sb = sem("qk_mm"), sem("v_mm"), sem("v_sb")
        soft_a, soft_sum = sem("soft_a"), sem("soft_sum")
        qkt_mm, qk_sb = sem("qkt_mm"), sem("qk_sb")
        outer, cum, k1_mm = sem("outer"), sem("cum"), sem("k1_mm")
        state_mm, state_sb = sem("state_mm"), sem("state_sb")
        m_prod, m_red, m_rden, o_done = (sem(n) for n in ("m_prod", "m_red", "m_rden", "o_done"))
        oT_mm, oT_sb, a_mm, an_done, x1_done = (sem(n) for n in ("oT_mm", "oT_sb", "a_mm", "an_done", "x1_done"))
        x1_kept = pair("x1_kept")
        rows_done = sem("rows_done")
        x2T_mm, x2T_sb, logit_mm, route, etop_done, rank_mm = (
            sem(n) for n in ("x2T_mm", "x2T_sb", "logit_mm", "route", "etop_done", "rank_mm"))
        meta, slots, scattered = sem("meta"), sem("slots"), pair("scattered")
        table, pads_in = sem("table"), sem("pads_in")
        xg_in, we_done = [sem(f"xg_in{k}") for k in range(RING)], sem("we_done")
        gT_mm, gT_sb, h_mm, h_done, y_mm, y_done, dest_a, dest_done = (
            sem(n) for n in ("gT_mm", "gT_sb", "h_mm", "h_done", "y_mm", "y_done", "dest_a", "dest_done"))
        y_sent = [sem(f"y_sent{k}") for k in range(RING)]
        y_in, pc_done, yp_done, ys_done, yn_done, fin_done = (
            [sem(f"y_in{q}") for q in range(RING)], sem("pc_done"), sem("yp_done"), sem("ys_done"), sem("yn_done"), sem("fin_done"))
        stored = pair("stored")

        n_const = 2 * 16
        block = ctx.enter_context(nc.Block())

        def hold(eng, *waits):
            known = [(s, v if isinstance(v, int) else eng.to_reg(v)) for s, v in waits]
            eng.wait_ge(consts_in, n_const)
            for s, v in known:
                wait(eng, s, v)

        def tile_of(eng, j):
            return j * NT if isinstance(j, int) else eng.snap(j * NT)

        def stages(i, t, u):
            found = {}
            for name, lag in OFFSETS.items():
                j = i - lag
                if isinstance(i, int) and not 0 <= j < B + (name == "W"):
                    continue
                found[name] = (j, (u - lag) % 2, t + (u - lag) // 2)
            return found

        def run_steps(eng, step):
            for i in range(8):
                step(stages(i, i // 2, i % 2))
            with eng.Fori(4, B // 2) as t:
                for u in range(2):
                    step(stages(2 * t + u, t, u))
            for i in range(B, STEPS):
                step(stages(i, i // 2, i % 2))

        def run_tiles(eng, tile):
            for i in range(RING):
                tile(i, i, 0)
            with eng.Fori(1, MOE_TILES // RING) as t:
                for q in range(RING):
                    tile(RING * t + q, q, t)
            for i in range(MOE_TILES // RING * RING, MOE_TILES):
                tile(i, i % RING, i // RING)

        def h_ps(p, f):
            bank = (kv_ps[f // 2] if p == 0 else qk_ps[:, (f // 2) * 512:(f // 2 + 1) * 512])
            return bank[:, (f % 2) * T:(f % 2 + 1) * T]

        @block.sync
        def _(sp):
            sp.dma_start(xe[0][:], x_v[:, 0:NT, :]).then_inc(xe_in[0], 16)
            sp.dma_start(par[:], params).then_inc(consts_in, 16)
            sp.dma_start(pad_rows[:], pad).then_inc(consts_in, 16)
            sp.wait_ge(consts_in, n_const)
            sp.dma_start(bucket[E * CAP:E * CAP + T, :].rearrange("(p j) w -> p (j w)", p=P), pad_rows[:]
                         ).then_inc(pads_in, 16)

            def step(at):
                if "E" in at:
                    j, p, r = at["E"]
                    first = tile_of(sp, j)
                    wait(sp, xn_done, (j - 1) * NT)
                    if isinstance(j, int) and j == 0:
                        return
                    sp.dma_start(xe[p][:], x_v[:, bass.ds(first, NT), :]).then_inc(xe_in[p], 16)
                if "Q" in at:
                    j, p, r = at["Q"]
                    first = tile_of(sp, j)
                    wait(sp, x1_done, j + 1)
                    sp.dma_start(x1_all[:, bass.ds(first, NT), :], x1[p][:]).then_inc(x1_kept[p], 16)
                if "O" in at:
                    j, p, r = at["O"]
                    first = tile_of(sp, j)
                    wait(sp, x1_done, j - 1)
                    sp.dma_start(xr[p][:], x_v[:, bass.ds(first, NT), :]).then_inc(xr_in[p], 16)

            run_steps(sp, step)
            sp.wait_ge(table, 1)
            for e in range(E):
                end = sp.value_load(end_i[0:1, e:e + 1], min_val=e * CAP, max_val=e * CAP + N)
                sp.dma_start(bucket[bass.ds(end, T), :].rearrange("(p j) w -> p (j w)", p=P), pad_rows[:]
                             ).then_inc(pads_in, 16)
            sp.wait_ge(pads_in, 16 * (E + 1))
            sp.wait_ge(table, TABLE_OPS)
            for p in range(2):
                sp.wait_ge(scattered[p], (B // 2) * 2 * NT * 16)

            def load_rows(i, q, r):
                row = sp.value_load(row_i[0:1, bass.ds(i, 1)], min_val=0, max_val=E * CAP)
                wait(sp, gT_mm, i - RING + 1)
                wait(sp, dest_done, i - RING + 1)
                sp.dma_start(xg[q][:].rearrange("p j w -> p (j w)"),
                             bucket[bass.ds(row, T), :].rearrange("(p j) w -> p (j w)", p=P)).then_inc(xg_in[q], 16)

            run_tiles(sp, load_rows)
            for q in range(RING):
                sp.wait_ge(y_sent[q], (MOE_TILES - q + RING - 1) // RING * 32)

            def load_y(j, q):
                first = tile_of(sp, j)
                wait(sp, ys_done, (j - RING + 1) * NT)
                for k, y in enumerate((y0, y1)):
                    sp.dma_start(y[q][:], y_v[k, :, bass.ds(first, NT), :]).then_inc(y_in[q], 16)

            def store(j, p):
                first = tile_of(sp, j)
                sp.wait_ge(fin_done, j + 1)
                sp.dma_start(out_v[:, bass.ds(first, NT), :], fin[p]).then_inc(stored[p], 16)

            for j in range(RING):
                load_y(j, j)
            with sp.Fori(1, B // RING) as t:
                for q in range(RING):
                    load_y(RING * t + q, q)
                    store(RING * t + q - RING, q % 2)
            for j in range(B - RING, B):
                store(j, j % 2)
            for p in range(2):
                sp.wait_ge(stored[p], B // 2 * 16)

        def layer_norm_act(act, key, j):
            if key == "ar":
                wait(act, stat["a"], (min(j + 1, B) if isinstance(j, int) else j + 1) * 2 * NT)
                wait(act, stat["r"], j * 2 * NT)
            else:
                act.wait_ge(stat[key], j * 2 * NT + 2 * NT)
            wait(act, newton[key], j * 4)
            act.activation(nw[key][:, 0, :], mv[key][:, :, 1], ACT.Ln, bias=eps_t[:, 0:1]).then_inc(lnexp[key], 1)
            act.wait_ge(lnexp[key], j * 2 + 1)
            act.activation(nw[key][:, 1, :], nw[key][:, 0, :], ACT.Exp, scale=-0.5).then_inc(lnexp[key], 1)

        def sums(v, key, tiles):
            for c in range(NT):
                v.bn_stats(st[key][:, c, :], tiles(c)).then_inc(stat[key], 1)

        def means(v, key, j, *read):
            hold(v, (stat[key], j * 2 * NT + NT), *read)
            for c in range(NT):
                v.bn_aggr(mv[key][:, c, :], st[key][:, c, :]).then_inc(stat[key], 1)

        def layer_norm_newton(v, key, j, between=None):
            a = nw[key]

            def other(tiles):
                if between:
                    for c in tiles:
                        v.bn_stats(st[between[0]][:, c, :], between[1](c)).then_inc(stat[between[0]], 1)

            v.wait_ge(lnexp[key], j * 2 + 2)
            v.scalar_tensor_tensor(a[:, 2, :], mv[key][:, :, 1], EPS, a[:, 1, :], ALU.add, ALU.mult
                                   ).then_inc(newton[key], 1)
            other((0, 1))
            v.wait_ge(newton[key], j * 4 + 1)
            v.scalar_tensor_tensor(a[:, 3, :], a[:, 2, :], -0.5, a[:, 1, :], ALU.mult, ALU.mult
                                   ).then_inc(newton[key], 1)
            other((2,))
            v.wait_ge(newton[key], j * 4 + 2)
            v.scalar_tensor_tensor(a[:, 4, :], a[:, 3, :], 1.5, a[:, 1, :], ALU.add, ALU.mult
                                   ).then_inc(newton[key], 1)
            other((3,))
            v.wait_ge(newton[key], j * 4 + 3)
            v.scalar_tensor_tensor(a[:, 5, :], mv[key][:, :, 0], -1.0, a[:, 4, :], ALU.mult, ALU.mult
                                   ).then_inc(newton[key], 1)

        @block.scalar
        def _(act):
            act.preload_act_table_set("natural_log_exp_and_others")
            act.wait_ge(init, 5)
            act.dma_start(W[:], wexp).then_inc(w_in, 16)
            act.wait_ge(bias_mm, 1)
            act.activation(attn_bias[:], st_ps[0:1, 0:D], ACT.Copy).then_inc(init_a, 1)

            def normalise(key, first, dst, src, done):
                for c in range(NT):
                    n = first + c
                    act.activation(dst(c), src(c), ACT.Identity, bias=nw[key][:, 5, n:n + 1],
                                   scale=nw[key][:, 4, n:n + 1]).then_inc(done, 1)

            def step(at):
                E_, F, O, Q, W_, R = (at.get(k) for k in "EFOQWR")
                if F:
                    j, p, r = F
                    act.wait_ge(qk_mm, j + 1)
                    wait(act, soft_sum, j)
                    for k in range(2):
                        act.activation(f_abs[:, k * S:(k + 1) * S], qk_ps[:, k * S:(k + 1) * S], ACT.Abs,
                                       bias=b_qk[:, k:k + 1]).then_inc(soft_a, 1)
                    for k in range(2):
                        act.activation(f_relu[:, k * S:(k + 1) * S], qk_ps[:, k * S:(k + 1) * S], ACT.Relu,
                                       bias=b_qk[:, k:k + 1]).then_inc(soft_a, 1)
                if W_:
                    layer_norm_act(act, "ar", W_[0])
                if F:
                    act.wait_ge(soft_a, j * 6 + 2)
                    act.activation(f_exp[:], f_abs[:], ACT.Exp, scale=-1.0).then_inc(soft_a, 1)
                    act.wait_ge(soft_a, j * 6 + 5)
                    act.activation(f_ln[:], f_exp[:], ACT.Ln, bias=1.0).then_inc(soft_a, 1)
                    act.wait_ge(v_mm, j + 1)
                    wait(act, outer, (j - 1) * NT)
                    wait(act, state_mm, (j - 1) * (NT - 1))
                    act.activation(vx[p][:].rearrange("p c (h w) -> p c h w", w=DEN)[:, :, :, 0:DH],
                                   xv_ps[:].rearrange("p (c h e) -> p c h e", c=NT, h=H), ACT.Copy).then_inc(v_sb, 1)
                if W_:
                    act.wait_ge(newton["ar"], W_[0] * 4 + 4)
                if Q:
                    j, p, r = Q
                    wait(act, x1_done, j)
                    normalise("ar", 0, lambda c: an[:, c, :], lambda c: out_ps[:, c * D:(c + 1) * D], an_done)
                if R:
                    j, p, r = R
                    wait(act, scattered[p], r * 2 * NT * 16)
                    normalise("ar", NT, lambda c: rows[p][:, c, 0:D], lambda c: x1[p][:, c, :], rows_done)
                    act.wait_ge(x2T_mm, j + 1)
                    wait(act, logit_mm, j)
                    act.activation(xn2T[:], out_ps[:], ACT.Copy).then_inc(x2T_sb, 1)
                if E_:
                    layer_norm_act(act, "e", E_[0])
                if F:
                    j, p, r = F
                    act.wait_ge(qkt_mm, j + 1)
                    wait(act, cum, (j - 1) * NT * 2)
                    wait(act, m_prod, (j - 1) * PRODS[NT])
                    for k in range(2):
                        act.activation(qk[p][:, 2 * k:2 * k + 2, :].rearrange("p c w -> p (c w)"),
                                       qk_ps[:, k * 512:(k + 1) * 512], ACT.Copy).then_inc(qk_sb, 1)
                if O:
                    j, p, r = O
                    act.wait_ge(oT_mm, j + 1)
                    wait(act, a_mm, j)
                    act.activation(oT[:], out_ps[:], ACT.Copy).then_inc(oT_sb, 1)
                if E_:
                    j, p, r = E_
                    act.wait_ge(newton["e"], j * 4 + 4)
                    wait(act, xnT_mm, j - 1)
                    normalise("e", 0, lambda c: xn[p][:, c, :], lambda c: xe[p][:, c, :], xn_done)
                if R:
                    j, p, r = R
                    act.wait_ge(route, j * 13 + 9)
                    wait(act, route, (j - 1) * 13 + 13)
                    act.activation(etop[:], dtop[:], ACT.Exp).then_inc(etop_done, 1)
                if E_:
                    j, p, r = E_
                    act.wait_ge(xnT_mm, j + 1)
                    wait(act, v_mm, j)
                    act.activation(xnT[:], xv_ps[:], ACT.Copy).then_inc(xnT_sb, 1)
            run_steps(act, step)

            act.preload_act_table(ACT.Gelu_apprx_tanh)
            def tile(i, q, r):
                p = q % 2
                act.wait_ge(gT_mm, i + 1)
                wait(act, h_mm, (i - 1) * FC)
                act.activation(xgT[p], gT_ps[p][:, 0:T], ACT.Copy).then_inc(gT_sb, 1)
                if not (isinstance(i, int) and i == 0):
                    gelu(i - 1, (q - 1) % RING)

            def gelu(i, q):
                p = q % 2
                for f in range(FC):
                    if f % 2 == 0:
                        act.wait_ge(h_mm, i * FC + f + 2)
                    if f == 0:
                        wait(act, y_mm, i - 1)
                    act.activation(hid[p][:, f, :], h_ps(p, f), ACT.Gelu_apprx_tanh,
                                   bias=we[q][:, 2 * FF + f:2 * FF + f + 1]).then_inc(h_done, 1)

            run_tiles(act, tile)
            gelu(MOE_TILES - 1, (MOE_TILES - 1) % RING)

            act.preload_act_table_set("natural_log_exp_and_others")

            def scale_first(j, q, r):
                p = q % 2
                act.wait_ge(pc_done, j + 1)
                act.wait_ge(y_in[q], r * 32 + 32)
                wait(act, ys_done, (j - 1) * NT)
                for c in range(NT):
                    act.activation(yp[p][:, c, :], y0[q][:, c, :], ACT.Copy, scale=pc[p][:, 2 * c:2 * c + 1]
                                   ).then_inc(yp_done, 1)

            def last(j, q, r, more=True):
                p = q % 2
                layer_norm_act(act, "c", j)
                if more:
                    scale_first(j + 2, (q + 2) % RING, r + (q + 2) // RING)
                act.wait_ge(newton["c"], j * 4 + 4)
                wait(act, fin_done, j - 1)
                for c in range(NT):
                    act.activation(yn[p][:, c, :], ys[q][:, c, :], ACT.Identity,
                                   bias=nw["c"][:, 5, c:c + 1], scale=nw["c"][:, 4, c:c + 1]).then_inc(yn_done, 1)

            for j in range(2):
                scale_first(j, j, 0)
            for j in range(RING):
                last(j, j, 0)
            with act.Fori(1, B // RING - 1) as t:
                for q in range(RING):
                    last(RING * t + q, q, t)
            for j in range(B - RING, B):
                last(j, j % RING, j // RING, j < B - 2)

        @block.tensor
        def _(pe):
            pe.wait_ge(consts_in, n_const)
            pe.matmul(st_ps[0:1, 0:D], b_v, w_o, start=True, stop=False)
            pe.wait_ge(init, 5)
            pe.matmul(st_ps[0:1, 0:D], ones_row[0:1, 0:1], b_o, start=False, stop=True).then_inc(bias_mm, 1)
            pe.wait_ge(init_a, 1)

            def prefix(at, c):
                if "M" not in at:
                    return
                j, p, r = at["M"]
                n = j * NT + c
                before = j * PRODS[NT] + PRODS[c]
                qt, kt = qk[p][:, c, 0:D], qk[p][:, c, D:2 * D]
                if c == 0:
                    pe.wait_ge(v_sb, j + 1)
                    pe.wait_ge(qk_sb, j * 2 + 2)
                wait(pe, m_prod, before - 2)
                m = pe.matmul(k1_ps, tri_s, kt, start=True, stop=True)
                if c > 0:
                    wait(pe, state_sb, j * (NT - 1) + c)
                    m = pe.matmul(inter_ps, qkT[p][:, c * P:(c + 1) * P], state[(c - 1) % 2][:], start=True, stop=True)
                m.then_inc(k1_mm, 1)
                pe.wait_ge(outer, n + 1)
                for k in range(2):
                    wait(pe, m_prod, before - 1 + k)
                    pe.matmul(kv_ps[k][:], tri_s, kv[c % 2][:, k * 512:(k + 1) * 512], start=True, stop=True
                              ).then_inc(cum, 1)
                if c < NT - 1:
                    wait(pe, state_sb, j * (NT - 1) + c)
                    if c == 0:
                        wait(pe, slots, (j - OFFSETS["R"] + OFFSETS["M"] - 1) * 7 + 4)
                    pe.matmul(st_ps[:, 0:HV], kt, vx[p][:, c, :], start=(c == 0), stop=True,
                              skip_group_check=True).then_inc(state_mm, 1)

            def step(at):
                E_, F, M, O, R = (at.get(k) for k in "EFMOR")
                if F:
                    j, p, r = F
                    pe.wait_ge(xnT_sb, j + 1)
                    wait(pe, qk_sb, j * 2)
                    for k in range(2):
                        m = pe.matmul(qk_ps[:, k * S:(k + 1) * S], w_qkv[:, k * D:(k + 1) * D], xnT[:],
                                      start=True, stop=True)
                    m.then_inc(qk_mm, 1)
                    for c in range(NT):
                        m = pe.matmul(xv_ps[:, c * D:(c + 1) * D], xnT[:, c * P:(c + 1) * P], w_qkv[:, 2 * D:3 * D],
                                      start=True, stop=True)
                    m.then_inc(v_mm, 1)
                prefix(at, 0)
                prefix(at, 1)
                prefix(at, 2)
                if R:
                    j, p, r = R
                    pe.wait_ge(rows_done, j * NT + NT)
                    wait(pe, an_done, (min(j + 2, B) if isinstance(j, int) else j + 2) * NT)
                    for c in range(NT):
                        m = pe.transpose(out_ps[:, c * P:(c + 1) * P], rows[p][:, c, 0:D], idn)
                    m.then_inc(x2T_mm, 1)
                if F:
                    j, p, r = F
                    pe.wait_ge(soft_sum, j + 1)
                    for c in range(NT):
                        for k in range(2):
                            m = pe.transpose(qk_ps[:, (2 * c + k) * P:(2 * c + k + 1) * P],
                                             qkT[p][:, k * S + c * P:k * S + (c + 1) * P], idn)
                    m.then_inc(qkt_mm, 1)
                if R:
                    j, p, r = R
                    pe.wait_ge(x2T_sb, j + 1)
                    wait(pe, slots, (j - 1) * 7 + 4)
                    if M:
                        pe.wait_ge(state_sb, M[0] * (NT - 1) + NT - 1)
                    for c in range(NT):
                        m = pe.matmul(logit_ps[:, c, :], xn2T[:, c * P:(c + 1) * P], w_gate, start=True, stop=True)
                    m.then_inc(logit_mm, 1)
                if O:
                    j, p, r = O
                    pe.wait_ge(o_done, j + 1)
                    wait(pe, an_done, j * NT)
                    for c in range(NT):
                        m = pe.transpose(out_ps[:, c * P:(c + 1) * P], o[p][:, c, :], idn)
                    m.then_inc(oT_mm, 1)
                prefix(at, 3)
                if E_:
                    j, p, r = E_
                    pe.wait_ge(xn_done, j * NT + NT)
                    wait(pe, v_sb, j)
                    for c in range(NT):
                        m = pe.transpose(xv_ps[:, c * P:(c + 1) * P], xn[p][:, c, :], idn)
                    m.then_inc(xnT_mm, 1)
                if O:
                    j, p, r = O
                    pe.wait_ge(oT_sb, j + 1)
                    for c in range(NT):
                        pe.matmul(out_ps[:, c * D:(c + 1) * D], ones_row[:], attn_bias[:], start=True, stop=False)
                        m = pe.matmul(out_ps[:, c * D:(c + 1) * D], oT[:, c * P:(c + 1) * P], w_o,
                                      start=False, stop=True)
                    m.then_inc(a_mm, 1)
                if R:
                    j, p, r = R
                    pe.wait_ge(route, j * 13 + 12)
                    for c in range(NT):
                        pe.matmul(rank_ps[:, c, :], tri_b[:], hot_b[:, c, :], start=True, stop=(c == 0))
                        for b in range(c):
                            pe.matmul(rank_ps[:, c, :], ones_b[:], hot_b[:, b, :], start=False, stop=(b == c - 1))
                    for c in range(NT):
                        m = pe.matmul(count_ps, ones_b[:], hot_b[:, c, :], start=(c == 0), stop=(c == NT - 1))
                    m.then_inc(rank_mm, 1)

            run_steps(pe, step)

            def rows_T(i, q, r):
                pe.wait_ge(xg_in[q], r * 16 + 16)
                wait(pe, gT_sb, i - 1)
                for k in range(2):
                    m = pe.transpose(gT_ps[q % 2][:, k * P:(k + 1) * P], xg[q][:, k, 0:D], idn)
                m.then_inc(gT_mm, 1)

            def up(i, q):
                p = q % 2
                pe.wait_ge(gT_sb, i + 1)
                pe.wait_ge(we_done, i + 1)
                wait(pe, h_done, (i - 1) * FC)
                for f in range(FC):
                    pe.matmul(h_ps(p, f), we[q][:, f * P:(f + 1) * P], xgT[p], start=True, stop=True).then_inc(h_mm, 1)

            def down(i, q):
                p = q % 2
                pe.wait_ge(h_done, i * FC + FC)
                wait(pe, y_done, i - 1)
                for k in range(2):
                    for f in range(FC):
                        m = pe.matmul(y_ps[p][:, k * D:(k + 1) * D], hid[p][:, f, k * P:(k + 1) * P],
                                      we[q][:, FF + f * D:FF + (f + 1) * D], start=(f == 0), stop=(f == FC - 1))
                m.then_inc(y_mm, 1)

            pe.wait_ge(an_done, B * NT)
            pe.wait_ge(x2T_sb, B)
            pe.wait_ge(slots, B * 7)
            pe.wait_ge(m_prod, B * PRODS[NT])

            def tile(i, q, r):
                rows_T(i, q, r)
                if not (isinstance(i, int) and i < 1):
                    up(i - 1, (q - 1) % RING)
                if not (isinstance(i, int) and i < 2):
                    down(i - 2, (q - 2) % RING)

            run_tiles(pe, tile)
            up(MOE_TILES - 1, (MOE_TILES - 1) % RING)
            for i in range(MOE_TILES - 2, MOE_TILES):
                down(i, i % RING)

        @block.vector
        def _(v):
            v.memset(eps_t[:], EPS).then_inc(init, 1)
            v.memset(ones_row[:], 1.0).then_inc(init, 1)
            v.memset(ones_b[:], 1.0).then_inc(init, 1)
            for k in range(2):
                v.memset(vx[k][:].rearrange("p c (h w) -> p (c h) w", w=DEN)[:, :, DH:DEN], 1.0)
            v.memset(rows[0][:, :, D:RW], 0.0)
            v.memset(rows[1][:, :, D:RW], 0.0)
            v.memset(mv["ar"][:], 0.0)
            v.wait_ge(consts_in, n_const)
            v.tensor_copy(tri_b[:], tri_strict).then_inc(init, 1)
            v.tensor_copy(base[:], ecap).then_inc(init, 1)
            v.tensor_copy(token[:], tok0).then_inc(init, 1)
            v.wait_ge(init, 6)

            def products(at, c):
                if "M" not in at:
                    return
                j, p, r = at["M"]
                n = j * NT + c
                to = prod[c % 2]
                q = qk[p][:, c, 0:D].rearrange("p (h d) -> p h d", h=H)
                v.wait_ge(k1_mm, n + 1)
                wait(v, m_red, n - 1)
                v.tensor_tensor(to[:, :, 0:DH, DH], k1_ps.rearrange("p (h d) -> p h d", h=H), q, ALU.mult
                                ).then_inc(m_prod, 1)
                if c > 0:
                    v.tensor_copy(to[:, :, DH, :], inter_ps.rearrange("p (h w) -> p h w", h=H)).then_inc(m_prod, 1)
                for k in range(2):
                    hs = slice(k * 8, k * 8 + 8)
                    v.wait_ge(cum, 2 * n + k + 1)
                    v.tensor_tensor(to[:, hs, 0:DH, 0:DH],
                                    kv_ps[k][:].rearrange("p (h d e) -> p h d e", h=8, d=DH),
                                    q[:, hs, :, None].broadcast_to((P, 8, DH, DH)), ALU.mult).then_inc(m_prod, 1)
                if c < NT - 1:
                    v.wait_ge(state_mm, j * (NT - 1) + c + 1)
                    v.tensor_tensor(state[c % 2][:], st_ps[:, 0:HV], head_mask, ALU.mult).then_inc(state_sb, 1)

            def summed(at, c):
                if "M" not in at:
                    return
                j, p, r = at["M"]
                v.wait_ge(m_prod, j * PRODS[NT] + PRODS[c + 1])
                parts = DEN if c > 0 else DH
                if c == 0:
                    wait(v, o_done, j)
                v.tensor_reduce(num[:, c], prod[c % 2][:, :, 0:parts, :].rearrange("p h d e -> p h e d"),
                                AX, ALU.add).then_inc(m_red, 1)

            def step(at):
                E_, M, O, Q, W_, R = (at.get(k) for k in "EMOQWR")
                products(at, 0)
                summed(at, 0)
                e_tiles = None
                if E_:
                    v.wait_ge(xe_in[E_[1]], E_[2] * 16 + 16)
                    e_tiles = ("e", lambda c: xe[E_[1]][:, c, :])
                if W_:
                    layer_norm_newton(v, "ar", W_[0], e_tiles)
                elif E_:
                    sums(v, *e_tiles)
                if E_:
                    means(v, "e", E_[0])
                products(at, 1)
                summed(at, 1)
                products(at, 2)
                summed(at, 2)
                r_tiles = None
                if Q:
                    v.wait_ge(x1_done, Q[0] + 1)
                    r_tiles = ("r", lambda c: x1[Q[1]][:, c, :])
                if E_:
                    layer_norm_newton(v, "e", E_[0], r_tiles)
                elif Q:
                    sums(v, *r_tiles)
                if R:
                    j, p, r = R
                    n0 = j * 13
                    v.wait_ge(logit_mm, j + 1)
                    v.tensor_copy(logit[:], logit_ps).then_inc(route, 1)
                if R:
                    hold(v, (route, n0 + 1))
                    for c in range(NT):
                        v.max(top[:, c, :], logit[:, c, :]).then_inc(route, 1)
                if Q:
                    means(v, "r", Q[0])
                if R:
                    hold(v, (route, n0 + 5), (etop_done, j))
                    for c in range(NT):
                        m = v.max_index(topi[:, c, :], top[:, c, :], logit[:, c, :])
                        m.then_inc(route if c < NT - 1 else meta, 1)
                    v.tensor_tensor(dtop[:], top[:], top[:, :, 0:1].broadcast_to((P, NT, E)), ALU.subtract
                                    ).then_inc(route, 1)
                    v.wait_ge(meta, j * 4 + 1)
                    v.tensor_copy(topf[:], topi[:, :, 0:2]).then_inc(route, 1)
                    v.wait_ge(route, n0 + 10)
                    v.tensor_tensor(hot[:], iota8[:, None, None, :].broadcast_to((P, NT, 2, E)),
                                    topf[:, :, :, None].broadcast_to((P, NT, 2, E)), ALU.is_equal).then_inc(route, 1)
                    wait(v, scattered[p], r * 2 * NT * 16)
                    v.tensor_copy(rows[p][:, :, D + 1], topf[:, :, 0]).then_inc(meta, 1)
                    v.tensor_copy(rows[p][:, :, D], token[:]).then_inc(meta, 1)
                    v.wait_ge(route, n0 + 11)
                    wait(v, rank_mm, j)
                    v.tensor_tensor(hot_b[:], hot[:, :, 0, :], hot[:, :, 1, :], ALU.add).then_inc(route, 1)
                    v.wait_ge(meta, j * 4 + 3)
                    v.tensor_scalar(token[:], token[:], float(S), None, ALU.add).then_inc(meta, 1)
                products(at, 3)
                summed(at, 3)
                if R:
                    j, p, r = R
                    first = tile_of(v, j)
                    v.wait_ge(etop_done, j + 1)
                    v.tensor_reduce(zsum[:], etop[:], AX, ALU.add).then_inc(slots, 1)
                if M:
                    v.wait_ge(m_red, M[0] * NT + NT)
                    v.reciprocal(rden[:], num[:, :, :, DH]).then_inc(m_rden, 1)
                if R:
                    v.wait_ge(slots, j * 7 + 1)
                    v.reciprocal(rz[:], zsum[:]).then_inc(slots, 1)
                if M:
                    mj, mp, mr = M
                    v.wait_ge(m_rden, mj + 1)
                    wait(v, oT_mm, mj - 1)
                    v.tensor_tensor(o[mp][:].rearrange("p c (h e) -> p c h e", h=H), num[:, :, :, 0:DH],
                                    rden[:, :, :, None].broadcast_to((P, NT, H, DH)), ALU.mult).then_inc(o_done, 1)
                if R:
                    n0 = j * 7
                    v.wait_ge(slots, n0 + 2)
                    v.tensor_tensor(prob_all[:, bass.ds(first, NT), :],
                                    etop[:, :, 0:2], rz[:, :, None].broadcast_to((P, NT, 2)), ALU.mult
                                    ).then_inc(route, 1)
                    v.wait_ge(rank_mm, j + 1)
                    v.tensor_tensor(pos[:], rank_ps, base[:, None, :].broadcast_to((P, NT, E)), ALU.add
                                    ).then_inc(slots, 1)
                    v.wait_ge(slots, n0 + 3)
                    v.tensor_tensor(base[:], base[:], count_ps, ALU.add).then_inc(slots, 1)
                    v.tensor_tensor(psel[:], hot[:], pos[:, :, None, :].broadcast_to((P, NT, 2, E)), ALU.mult
                                    ).then_inc(slots, 1)
                if O:
                    v.wait_ge(a_mm, O[0] + 1)
                    sums(v, "a", lambda c: out_ps[:, c * D:(c + 1) * D])
                if R:
                    v.wait_ge(slots, n0 + 5)
                    v.tensor_reduce(slotf[:].rearrange("p (c k) -> p c k", k=2), psel[:], AX, ALU.add
                                    ).then_inc(slots, 1)
                if O:
                    means(v, "a", O[0])
                if R:
                    v.wait_ge(slots, n0 + 6)
                    wait(v, scattered[p], r * 2 * NT * 16)
                    v.tensor_copy(slot[p][:], slotf[:]).then_inc(slots, 1)

            run_steps(v, step)

            tn = [0]

            def t_op(ins):
                tn[0] += 1
                ins.then_inc(table, 1)
                v.wait_ge(table, tn[0])

            v.wait_ge(slots, B * 7)
            t_op(v.tensor_copy(end_i[:], base[:]))
            t_op(v.tensor_tensor(cnt[:], base[:], ecap, ALU.subtract))
            t_op(v.tensor_tensor(cmp32[:], cnt[:, :, None].broadcast_to((P, E, 32)),
                                 m256[:, None, :].broadcast_to((P, E, 32)), ALU.is_gt))
            t_op(v.tensor_reduce(ntile[:], cmp32[:], AX, ALU.add))
            t_op(v.tensor_tensor(trie[:], lower, ntile[:, None, :].broadcast_to((P, E, E)), ALU.mult))
            t_op(v.tensor_reduce(tend[:], trie[:], AX, ALU.add))
            t_op(v.tensor_tensor(ge[:], tnum[:, :, None].broadcast_to((P, MOE_TILES, E)),
                                 tend[:, None, :].broadcast_to((P, MOE_TILES, E)), ALU.is_ge))
            t_op(v.tensor_reduce(ex_of[:], ge[:], AX, ALU.add))
            t_op(v.tensor_tensor(gen[:], ge[:], ntile[:, None, :].broadcast_to((P, MOE_TILES, E)), ALU.mult))
            t_op(v.tensor_reduce(t_start[:], gen[:], AX, ALU.add))
            t_op(v.tensor_tensor(row_of[:], tnum, t_start[:], ALU.subtract))
            t_op(v.tensor_scalar(row_b[:], row_of[:], float(T), None, ALU.mult))
            t_op(v.scalar_tensor_tensor(row_of[:], ex_of[:], float(CAP), row_b[:], ALU.mult, ALU.add))
            t_op(v.tensor_scalar(row_b[:], row_of[:], float(E * CAP), None, ALU.min))
            t_op(v.tensor_copy(row_i[:], row_b[:]))
            t_op(v.tensor_scalar(ex_min[:], ex_of[:], float(E - 1), None, ALU.min))
            t_op(v.tensor_copy(ex_i[:], ex_min[:]))
            assert tn[0] == TABLE_OPS
            v.wait_ge(w_in, 16)

            def tile(i, q, r):
                e = v.value_load(ex_i[0:1, bass.ds(i, 1)], min_val=0, max_val=E - 1)
                hold(v, (y_done, i - RING + 1))
                v.tensor_copy(we[q][:], W[:, bass.ds(e, 1), :].rearrange("p a w -> p (a w)")).then_inc(we_done, 1)
                v.wait_ge(we_done, i + 1)
                v.wait_ge(xg_in[q], r * 16 + 16)
                v.tensor_scalar(second[q][:], xg[q][:, :, D + 1], we[q][:, WW - 2:WW - 1], float(N),
                                ALU.not_equal, ALU.mult).then_inc(dest_a, 1)
                v.wait_ge(dest_a, i + 1)
                wait(v, y_sent[q], r * 32)
                v.tensor_tensor(dest[q][:], second[q][:], xg[q][:, :, D], ALU.add).then_inc(dest_done, 1)
                if not (isinstance(i, int) and i < 2):
                    finish(i - 2, (q - 2) % RING, r - (q < 2))

            def finish(i, q, r):
                v.wait_ge(y_mm, i + 1)
                wait(v, y_sent[q], r * 32)
                v.tensor_tensor(yv[q][:], y_ps[q % 2][:, 0:T].rearrange("p (k d) -> p k d", k=2),
                                we[q][:, None, 2 * FF + FC:2 * FF + FC + D].broadcast_to((P, 2, D)), ALU.add
                                ).then_inc(y_done, 1)

            run_tiles(v, tile)
            for i in range(MOE_TILES - 2, MOE_TILES):
                finish(i, i % RING, i // RING)

            def weights(j, p):
                first = tile_of(v, j)
                hold(v, (ys_done, (j - 1) * NT), (yp_done, (j - 1) * NT))
                v.tensor_copy(pc[p][:], prob_all[:, bass.ds(first, NT), :].rearrange("p c k -> p (c k)")
                              ).then_inc(pc_done, 1)

            def last(j, q, r):
                p = q % 2
                if not (isinstance(j, int) and j == B - 1):
                    weights(j + 1, 1 - p)
                v.wait_ge(pc_done, j + 1)
                v.wait_ge(y_in[q], r * 32 + 32)
                wait(v, yn_done, (j - RING + 1) * NT)
                for c in range(NT):
                    v.wait_ge(yp_done, j * NT + c + 1)
                    v.scalar_tensor_tensor(ys[q][:, c, :], y1[q][:, c, :], pc[p][:, 2 * c + 1:2 * c + 2],
                                           yp[p][:, c, :], ALU.mult, ALU.add).then_inc(ys_done, 1)
                v.wait_ge(ys_done, j * NT + NT)
                if isinstance(j, int) and j == 0:
                    sums(v, "c", lambda c: ys[q][:, c, :])
                else:
                    layer_norm_newton(v, "c", j - 1, ("c", lambda c: ys[q][:, c, :]))
                means(v, "c", j, (newton["c"], j * 4))

            for p in range(2):
                v.wait_ge(x1_kept[p], B // 2 * 16)
            weights(0, 0)
            for j in range(RING):
                last(j, j, 0)
            with v.Fori(1, B // RING - 1) as t:
                for q in range(RING):
                    last(RING * t + q, q, t)
            for j in range(B - RING, B):
                last(j, j % RING, j // RING)
            layer_norm_newton(v, "c", B - 1)

        @block.gpsimd
        def _(gp):
            gp.wait_ge(init, 6)

            def outer_product(at, c):
                if at:
                    j, p, r = at
                    if c == 0:
                        gp.wait_ge(qk_sb, j * 2 + 2)
                        gp.wait_ge(v_sb, j + 1)
                    wait(gp, cum, (j * NT + c - 1) * 2)
                    gp.tensor_tensor(
                        kv[c % 2][:].rearrange("p (h d e) -> p h d e", h=H, d=DH),
                        qk[p][:, c, D:2 * D].rearrange("p (h d) -> p h d", h=H)[:, :, :, None]
                        .broadcast_to((P, H, DH, DH)),
                        vx[p][:, c, :].rearrange("p (h w) -> p h w", w=DEN)[:, :, None, 0:DH]
                        .broadcast_to((P, H, DH, DH)), ALU.mult).then_inc(outer, 1)

            def scatter(at, choices):
                j, p, r = at
                for n in choices:
                    gp.indirect_dma_start(
                        out=bucket, out_offset=bass.IndirectOffsetOnAxis(ap=slot[p][:, n:n + 1], axis=0),
                        in_=rows[p][:, n // 2, :], in_offset=None).then_inc(scattered[p], 16)

            def step(at):
                F, M, Q, S_ = (at.get(k) for k in "FMQS")
                outer_product(M, 2)
                if F:
                    j, p, r = F
                    gp.wait_ge(soft_a, j * 6 + 6)
                    wait(gp, qkt_mm, j - 1)
                    wait(gp, cum, (j - 1) * NT * 2)
                    gp.tensor_tensor(qkT[p][:], f_ln[:], f_relu[:], ALU.add).then_inc(soft_sum, 1)
                outer_product(M, 3)
                if Q:
                    j, p, r = Q
                    gp.wait_ge(an_done, j * NT + NT)
                    gp.wait_ge(xr_in[p], r * 16 + 16)
                    wait(gp, x1_kept[p], r * 16)
                    wait(gp, rows_done, (j - 1) * NT)
                    gp.tensor_tensor(x1[p][:], an[:], xr[p][:], ALU.add).then_inc(x1_done, 1)
                if S_:
                    hold(gp, (slots, S_[0] * 7 + 7), (meta, S_[0] * 4 + 4), (rows_done, S_[0] * NT + NT))
                    scatter(S_, range(0, 3))
                outer_product(F, 0)
                if S_:
                    scatter(S_, range(3, 6))
                outer_product(F, 1)
                if S_:
                    scatter(S_, range(6, 2 * NT))

            run_steps(gp, step)

            def send(i, q, r):
                hold(gp, (y_done, i + 1), (dest_done, i + 1))
                for k in range(2):
                    gp.indirect_dma_start(
                        out=ychoice, out_offset=bass.IndirectOffsetOnAxis(ap=dest[q][:, k:k + 1], axis=0),
                        in_=yv[q][:, k, :], in_offset=None, bounds_check=2 * N - 1, oob_is_err=False
                    ).then_inc(y_sent[q], 16)

            run_tiles(gp, send)

            for p in range(2):
                gp.wait_ge(x1_kept[p], B // 2 * 16)

            def last(j, p, r):
                first = tile_of(gp, j)
                hold(gp, (yn_done, j * NT + NT), (stored[p], r * 16))
                gp.tensor_tensor(fin[p], yn[p][:], x1_all[:, bass.ds(first, NT), :], ALU.add).then_inc(fin_done, 1)

            for j in range(2):
                last(j, j, 0)
            with gp.Fori(1, B // 2) as t:
                for p in range(2):
                    last(2 * t + p, p, t)


def kernel(**inputs):
    import numpy as np
    import concourse.bacc as bacc
    from concourse.bass_utils import run_bass_kernel_spmd as run

    a = {k.split("_", 1)[1]: np.asarray(v) for k, v in inputs.items()}
    f = np.float32
    w1 = a["ffn_w1"].transpose(2, 1, 0)
    w2 = a["ffn_w2"].reshape(D, E, FC, P).transpose(3, 1, 2, 0).reshape(P, E, FC * D)
    b1 = a["ffn_b1"].reshape(E, FC, P).transpose(2, 0, 1)
    b2 = np.broadcast_to(a["ffn_b2"][None], (P, E, D))
    number = np.zeros((P, E, 2), f)
    number[:, :, 0] = np.arange(E)
    pad = np.zeros((T, RW), f)
    pad[:, D] = N + np.arange(T)
    pad[:, D + 1] = -1
    consts = np.zeros((P, 188), f)
    consts[:, 0:E] = np.arange(E)
    consts[:, E:2 * E] = np.arange(E) * CAP
    consts[:, 16:48] = np.arange(32) * T
    consts[:, 48:112] = np.tril(np.ones((E, E))).reshape(-1)
    consts[:, 112:112 + MOE_TILES] = np.arange(MOE_TILES)
    consts[:, 183:187] = np.arange(P)[:, None] + P * np.arange(NT)[None]
    heads = np.arange(P) // DH
    mask = (heads[:, None] == np.arange(HV)[None] // DEN).astype(f)
    parts = {
        "ident": np.eye(P, dtype=f), "w_qkv": np.concatenate([a["attn_Wq"].T, a["attn_Wk"].T, a["attn_Wv"].T], 1),
        "b_qk": np.stack([a["attn_bq"], a["attn_bk"]], 1), "w_o": a["attn_Wo"].T, "w_gate": a["ffn_gate_w"].T,
        "b_v": a["attn_bv"][:, None], "b_o": np.broadcast_to(a["attn_bo"][None], (P, D)),
        "tri": np.triu(np.ones((P, P), f)), "tri_strict": np.triu(np.ones((P, P), f), 1),
        "mask": mask, "con": consts,
    }
    arrays = {
        "x": a["attn_x"], "params": np.concatenate([parts[k] for k in PARAMS], 1),
        "wexp": np.concatenate([w1, w2, b1, b2, number], 2), "pad": pad.reshape(P, 2 * RW),
    }
    arrays = {f"in_{k}": np.ascontiguousarray(v) for k, v in arrays.items()}
    nc = bacc.Bacc("TRN2", target_bir_lowering=False, num_devices=1)
    args = [nc.dram_tensor(k, v.shape, mybir.dt.from_np(v.dtype), kind="ExternalInput").ap() for k, v in arrays.items()]
    out = nc.dram_tensor("out_0", (B, S, D), F32, kind="ExternalOutput").ap()
    build(nc, *args, out)
    r = run(nc, [arrays], core_ids=[0])
    return r.results[0]["out_0"]
```

```python
from contextlib import ExitStack

import concourse.bass as bass
from concourse import mybir

F32 = mybir.dt.float32
F32R = mybir.dt.float32r
BF16 = mybir.dt.bfloat16
I32 = mybir.dt.int32
U32 = mybir.dt.uint32
ALU = mybir.AluOpType
ACT = mybir.ActivationFunctionType
AX = mybir.AxisListType.X

P = 128
B, S, D = 16, 512, 128
H, DH = 16, 8
NT = S // P
N = B * S
E, FF = 8, 512
FC = FF // P
DEN = DH + 1
HV = H * DEN
T = 256
CAP = N + T
RING = 4
MOE_TILES = (2 * N + E * (T - 1)) // T
RW = 132
B1_AT = FC * D
B2_AT = B1_AT + FC
NUMBER_AT = B2_AT + D
WW = NUMBER_AT + 2
EPS = 1e-5
OFFSETS = dict(E=0, F=1, M=2, O=3, Q=4, W=4, R=5, S=6)
STEPS = B + 6
TABLE_OPS = 17
PRODS = (0, 3, 7, 11, 15)

PARAMS = dict(ident=P, w_qkv=3 * D, b_qk=2, w_o=D, w_gate=E, b_v=1, b_o=D, tri=P, tri_strict=P, mask=HV, con=188)


def wait(eng, sem, value):
    if isinstance(value, int) and value <= 0:
        return
    eng.wait_ge(sem, value)


def build(nc, x, params, w1, wexp, pad, out):
    bucket = nc.dram_tensor("bucket", (E * CAP + T, RW), F32, kind="Internal").ap()
    ychoice = nc.dram_tensor("ychoice", (2 * N, D), F32, kind="Internal").ap()
    x_v = x.rearrange("b (c p) d -> p (b c) d", p=P)
    out_v = out.rearrange("b (c p) d -> p (b c) d", p=P)
    y_v = ychoice.rearrange("(k t p) d -> k p t d", k=2, p=P)

    with ExitStack() as ctx:
        def sb(name, shape, dt=F32):
            return ctx.enter_context(nc.sbuf_tensor(name, shape, dt))

        def ps(name, shape, dt=F32):
            return ctx.enter_context(nc.psum_tensor(name, shape, dt))

        def sem(name):
            return ctx.enter_context(nc.semaphore(name))

        def pair(name):
            return [sem(f"{name}{k}") for k in range(2)]

        par = sb("par", [P, sum(PARAMS.values())])
        at_col, part = 0, {}
        for name, width in PARAMS.items():
            part[name] = par[:, at_col:at_col + width]
            at_col += width
        w_qkv, w_o, w_gate, b_qk, b_v, idn, tri_s, tri_strict, head_mask, con = (
            part[k] for k in ("w_qkv", "w_o", "w_gate", "b_qk", "b_v", "ident", "tri", "tri_strict", "mask", "con"))
        b_o = part["b_o"][0:1, :]
        attn_bias = sb("attn_bias", [1, D])
        tri_b = sb("tri_b", [P, P], BF16)
        ones_b = sb("ones_b", [P, P], BF16)
        ones_row = sb("ones_row", [1, P])
        eps_t = sb("eps_t", [P, 1])
        W = sb("W", [P, E, WW])
        w1_parts = sb("w1_parts", [P, E, 2, FF], F32R)
        pad_rows = sb("pad_rows", [P, 2 * RW])
        xe = [sb(f"xe{k}", [P, NT, D]) for k in range(2)]
        xr = [sb(f"xr{k}", [P, NT, D]) for k in range(2)]
        xn = [sb(f"xn{k}", [P, NT, D]) for k in range(2)]
        xnT = sb("xnT", [P, S])
        f_abs = sb("f_abs", [P, 2 * S])
        f_exp = sb("f_exp", [P, 2 * S])
        f_ln = sb("f_ln", [P, 2 * S])
        f_relu = sb("f_relu", [P, 2 * S])
        qkT = [sb(f"qkT{k}", [P, 2 * S]) for k in range(2)]
        qk = [sb(f"qk{k}", [P, NT, 2 * D]) for k in range(2)]
        vx = [sb(f"vx{k}", [P, NT, HV]) for k in range(2)]
        kv = [sb(f"kv{k}", [P, H * DH * DH]) for k in range(2)]
        prod = [sb(f"prod{k}", [P, H, DEN, DEN]) for k in range(2)]
        num = sb("num", [P, NT, H, DEN])
        rden = sb("rden", [P, NT, H])
        state = [sb(f"state{k}", [P, HV]) for k in range(2)]
        o = [sb(f"o{k}", [P, NT, D]) for k in range(2)]
        oT = sb("oT", [P, S])
        an = sb("an", [P, NT, D])
        x1 = [sb(f"x1{k}", [P, NT, D]) for k in range(2)]
        rows = [sb(f"rows{k}", [P, NT, RW]) for k in range(2)]
        xn2T = sb("xn2T", [P, S])
        logit = sb("logit", [P, NT, E])
        top = sb("top", [P, NT, E])
        topi = sb("topi", [P, NT, E], U32)
        topf = sb("topf", [P, NT, 2])
        dtop = sb("dtop", [P, NT, E])
        etop = sb("etop", [P, NT, E])
        zsum = sb("zsum", [P, NT])
        rz = sb("rz", [P, NT])
        hot = sb("hot", [P, NT, 2, E])
        hot_b = sb("hot_b", [P, NT, E], BF16)
        base = sb("base", [P, E])
        pos = sb("pos", [P, NT, E])
        psel = sb("psel", [P, NT, 2, E])
        slotf = sb("slotf", [P, NT * 2])
        slot = [sb(f"slot{k}", [P, NT * 2], I32) for k in range(2)]
        token = sb("token", [P, NT])
        e_sum, e_squares, e_shift = (sb(n, [P, NT]) for n in ("e_sum", "e_squares", "e_shift"))
        st = {k: sb(f"st_{k}", [P, NT, 6]) for k in "arc"}
        mv = {"c": sb("mv_c", [P, NT, 2])}
        mv["ar"] = sb("mv_ar", [P, 2 * NT, 2])
        mv["a"], mv["r"] = mv["ar"][:, 0:NT, :], mv["ar"][:, NT:2 * NT, :]
        nw = {k: sb(f"nw_{k}", [P, 6, len(k) * NT]) for k in ("e", "ar", "c")}
        x1_all = sb("x1_all", [P, B * NT, D])
        w1_raw = x1_all[:, 0:E * FF // D, :].rearrange("p (e b) d -> p e (b d)", e=E)
        prob_all = sb("prob_all", [P, B * NT, 2])
        cnt = sb("cnt", [P, E])
        ntile = sb("ntile", [P, E])
        tend = sb("tend", [P, E])
        ge, gen = (t[:, 0:MOE_TILES * E].rearrange("p (i e) -> p i e", e=E) for t in (f_exp, f_ln))
        cmp32 = f_abs[:, 0:E * 32].rearrange("p (e b) -> p e b", e=E)
        trie = f_relu[:, 0:E * E].rearrange("p (a b) -> p a b", a=E)
        ex_of = sb("ex_of", [P, MOE_TILES])
        t_start = sb("t_start", [P, MOE_TILES])
        row_of = sb("row_of", [P, MOE_TILES])
        row_b = sb("row_b", [P, MOE_TILES])
        ex_min = sb("ex_min", [P, MOE_TILES])
        row_i = sb("row_i", [P, MOE_TILES], I32)
        ex_i = sb("ex_i", [P, MOE_TILES], I32)
        end_i = sb("end_i", [P, E], I32)
        xg = [t[:].rearrange("p c d -> p (c d)")[:, 0:2 * RW].rearrange("p (j w) -> p j w", j=2) for t in (*xe, *xn)]
        flat = [t[:].rearrange("p h a b -> p (h a b)") for t in prod]
        we = [flat[k // 2][:, k % 2 * WW:(k % 2 + 1) * WW] for k in range(RING)]
        we1 = [sb(f"we1_{k}", [P, 2 * FF], F32R) for k in range(2)]
        xgT_hi, xgT_lo = ([sb(f"xgT_{n}{k}", [P, T], F32R) for k in range(2)] for n in ("hi", "lo"))
        hid = [f[:].rearrange("p (f t) -> p f t", f=FC) for f in (f_exp, f_ln)]
        yv = [f_abs[:, k * T:(k + 1) * T].rearrange("p (k d) -> p k d", k=2) for k in range(RING)]
        second = [sb(f"second{k}", [P, 2]) for k in range(RING)]
        dest = [sb(f"dest{k}", [P, 2], I32) for k in range(RING)]
        y0, y1 = ([*t, *(q[:, k * S:(k + 1) * S].rearrange("p (c d) -> p c d", c=NT) for k in range(2))]
                  for t, q in ((xe, qkT[0]), (xr, qkT[1])))
        ys = [*x1, *(f_relu[:, k * S:(k + 1) * S].rearrange("p (c d) -> p c d", c=NT) for k in range(2))]
        yp, yn, fin = xn, o, [rows[k][:, :, 0:D] for k in range(2)]
        pc = [sb(f"pc{k}", [P, NT * 2]) for k in range(RING)]

        kv_ps = [ps(f"kv_ps{k}", [P, 512]) for k in range(2)]
        small = ps("small", [P, 512])
        st_ps = ps("st_ps", [P, 512])
        qk_ps = ps("qk_ps", [P, 1024])
        xv_ps = ps("xv_ps", [P, 512])
        out_ps = ps("out_ps", [P, 512])
        k1_ps = small[:, 0:D]
        inter_ps = small[:, D:D + HV]
        logit_ps, rank_ps = (st_ps[:, a:a + NT * E].rearrange("p (c e) -> p c e", c=NT) for a in (HV, HV + NT * E))
        count_ps = st_ps[:, HV + 2 * NT * E:HV + 2 * NT * E + E]
        gT_ps, y_ps = (xv_ps, st_ps), (out_ps, small)

        iota8 = con[:, 0:E]
        ecap = con[:, E:2 * E]
        m256 = con[:, 16:48]
        lower = con[:, 48:48 + E * E].rearrange("p (a b) -> p a b", a=E)
        tnum = con[:, 112:112 + MOE_TILES]
        tok0 = con[:, 183:183 + NT]

        consts_in, w_in, w1_hi, w1_lo = (sem(n) for n in ("consts_in", "w_in", "w1_hi", "w1_lo"))
        init, init_a = sem("init"), sem("init_a")
        bias_mm = sem("bias_mm")
        xe_in, xr_in = pair("xe_in"), pair("xr_in")
        stat = {k: sem(f"stat_{k}") for k in "earc"}
        lnexp = {k: sem(f"lnexp_{k}") for k in ("e", "ar", "c")}
        newton = {k: sem(f"newton_{k}") for k in ("e", "ar", "c")}
        xn_done = sem("xn_done")
        xnT_mm, xnT_sb = sem("xnT_mm"), sem("xnT_sb")
        qk_mm, v_mm, v_sb = sem("qk_mm"), sem("v_mm"), sem("v_sb")
        soft_a, soft_sum = sem("soft_a"), sem("soft_sum")
        qkt_mm, qk_sb = sem("qkt_mm"), sem("qk_sb")
        outer, cum, k1_mm = sem("outer"), sem("cum"), sem("k1_mm")
        state_mm, state_sb = sem("state_mm"), sem("state_sb")
        m_prod, m_red, m_rden, o_done = (sem(n) for n in ("m_prod", "m_red", "m_rden", "o_done"))
        oT_mm, oT_sb, a_mm, an_done, x1_done = (sem(n) for n in ("oT_mm", "oT_sb", "a_mm", "an_done", "x1_done"))
        x1_kept = pair("x1_kept")
        rows_done = sem("rows_done")
        x2T_mm, x2T_sb, logit_mm, route, etop_done, rank_mm = (
            sem(n) for n in ("x2T_mm", "x2T_sb", "logit_mm", "route", "etop_done", "rank_mm"))
        meta, slots, scattered = sem("meta"), sem("slots"), pair("scattered")
        table, pads_in = sem("table"), sem("pads_in")
        xg_in, we_done = [sem(f"xg_in{k}") for k in range(RING)], sem("we_done")
        gT_mm, gT_sb, gT_lo, h_mm, h_done, y_mm, y_done, dest_a, dest_done = (
            sem(n) for n in ("gT_mm", "gT_sb", "gT_lo", "h_mm", "h_done", "y_mm", "y_done", "dest_a", "dest_done"))
        y_sent = [sem(f"y_sent{k}") for k in range(RING)]
        y_in = [sem(f"y_in{q}") for q in range(RING)]
        pc_done, yp_done, ys_done, yn_done, fin_done = (
            sem(n) for n in ("pc_done", "yp_done", "ys_done", "yn_done", "fin_done"))
        stored = pair("stored")

        n_const = 2 * 16
        block = ctx.enter_context(nc.Block())

        def hold(eng, *waits):
            known = [(s, v if isinstance(v, int) else eng.to_reg(v)) for s, v in waits]
            eng.wait_ge(consts_in, n_const)
            for s, v in known:
                wait(eng, s, v)

        def tile_of(eng, j):
            return j * NT if isinstance(j, int) else eng.snap(j * NT)

        def stages(i, t, u):
            found = {}
            for name, lag in OFFSETS.items():
                j = i - lag
                if isinstance(i, int) and not 0 <= j < B + (name == "W"):
                    continue
                found[name] = (j, (u - lag) % 2, t + (u - lag) // 2)
            return found

        def run_steps(eng, step, after_second=lambda: None):
            for i in range(8):
                step(stages(i, i // 2, i % 2))
                if i == 1:
                    after_second()
            with eng.Fori(4, B // 2) as t:
                for u in range(2):
                    step(stages(2 * t + u, t, u))
            for i in range(B, STEPS):
                step(stages(i, i // 2, i % 2))

        def run_tiles(eng, tile):
            for i in range(RING):
                tile(i, i, 0)
            with eng.Fori(1, MOE_TILES // RING) as t:
                for q in range(RING):
                    tile(RING * t + q, q, t)
            for i in range(MOE_TILES // RING * RING, MOE_TILES):
                tile(i, i % RING, i // RING)

        def h_ps(p, f):
            bank = (kv_ps[f // 2] if p == 0 else qk_ps[:, (f // 2) * 512:(f // 2 + 1) * 512])
            return bank[:, (f % 2) * T:(f % 2 + 1) * T]

        @block.sync
        def _(sp):
            sp.dma_start(xe[0][:], x_v[:, 0:NT, :]).then_inc(xe_in[0], 16)
            sp.dma_start(par[:], params).then_inc(consts_in, 16)
            sp.dma_start(pad_rows[:], pad).then_inc(consts_in, 16)
            sp.wait_ge(consts_in, n_const)
            sp.dma_start(bucket[E * CAP:E * CAP + T, :].rearrange("(p j) w -> p (j w)", p=P), pad_rows[:]
                         ).then_inc(pads_in, 16)

            def step(at):
                if "E" in at:
                    j, p, r = at["E"]
                    if not (isinstance(j, int) and j == 0):
                        first = tile_of(sp, j)
                        wait(sp, xn_done, (j - 1) * NT)
                        sp.dma_start(xe[p][:], x_v[:, bass.ds(first, NT), :]).then_inc(xe_in[p], 16)
                if "Q" in at:
                    j, p, r = at["Q"]
                    first = tile_of(sp, j)
                    if isinstance(j, int) and j == 0:
                        sp.wait_ge(w1_lo, 2)
                    wait(sp, x1_done, j + 1)
                    sp.dma_start(x1_all[:, bass.ds(first, NT), :], x1[p][:]).then_inc(x1_kept[p], 16)
                if "O" in at:
                    j, p, r = at["O"]
                    first = tile_of(sp, j)
                    wait(sp, x1_done, j - 1)
                    sp.dma_start(xr[p][:], x_v[:, bass.ds(first, NT), :]).then_inc(xr_in[p], 16)

            run_steps(sp, step)
            sp.wait_ge(table, 1)
            for e in range(E):
                end = sp.value_load(end_i[0:1, e:e + 1], min_val=e * CAP, max_val=e * CAP + N)
                sp.dma_start(bucket[bass.ds(end, T), :].rearrange("(p j) w -> p (j w)", p=P), pad_rows[:]
                             ).then_inc(pads_in, 16)
            sp.wait_ge(pads_in, 16 * (E + 1))
            sp.wait_ge(table, TABLE_OPS)
            for p in range(2):
                sp.wait_ge(scattered[p], (B // 2) * 2 * NT * 16)

            def load_rows(i, q, r):
                row = sp.value_load(row_i[0:1, bass.ds(i, 1)], min_val=0, max_val=E * CAP)
                wait(sp, gT_mm, i - RING + 1)
                wait(sp, dest_done, i - RING + 1)
                sp.dma_start(xg[q].rearrange("p j w -> p (j w)"),
                             bucket[bass.ds(row, T), :].rearrange("(p j) w -> p (j w)", p=P)).then_inc(xg_in[q], 16)

            run_tiles(sp, load_rows)
            for q in range(RING):
                sp.wait_ge(y_sent[q], (MOE_TILES - q + RING - 1) // RING * 32)

            def load_y(j, q):
                first = tile_of(sp, j)
                wait(sp, ys_done, (j - RING + 1) * NT)
                for k, y in enumerate((y0, y1)):
                    sp.dma_start(y[q][:], y_v[k, :, bass.ds(first, NT), :]).then_inc(y_in[q], 16)

            def store(j, p):
                first = tile_of(sp, j)
                sp.wait_ge(fin_done, j + 1)
                sp.dma_start(out_v[:, bass.ds(first, NT), :], fin[p]).then_inc(stored[p], 16)

            for j in range(RING):
                load_y(j, j)
            with sp.Fori(1, B // RING) as t:
                for q in range(RING):
                    load_y(RING * t + q, q)
                    store(RING * t + q - RING, q % 2)
            for j in range(B - RING, B):
                store(j, j % 2)
            for p in range(2):
                sp.wait_ge(stored[p], B // 2 * 16)

        def guess(act, key, j):
            if key == "ar":
                wait(act, stat["a"], (min(j + 1, B) if isinstance(j, int) else j + 1) * 2 * NT)
                wait(act, stat["r"], j * 2 * NT)
            elif key == "e":
                act.wait_ge(stat["e"], j * 9 + 9)
            else:
                act.wait_ge(stat["c"], j * 2 * NT + 2 * NT)
            wait(act, newton[key], j * 4)
            var, scale = (e_squares[:], 1 / D) if key == "e" else (mv[key][:, :, 1], 1.0)
            act.activation(nw[key][:, 0, :], var, ACT.Ln, bias=eps_t[:, 0:1], scale=scale).then_inc(lnexp[key], 1)
            act.wait_ge(lnexp[key], j * 2 + 1)
            act.activation(nw[key][:, 1, :], nw[key][:, 0, :], ACT.Exp, scale=-0.5).then_inc(lnexp[key], 1)

        def tile_sums(v, key, c, tile):
            v.bn_stats(st[key][:, c, :], tile).then_inc(stat[key], 1)

        def means(v, key, j, *read):
            hold(v, (stat[key], j * 2 * NT + NT), *read)
            for c in range(NT):
                v.bn_aggr(mv[key][:, c, :], st[key][:, c, :]).then_inc(stat[key], 1)

        def newton_part(v, key, j, part):
            a = nw[key]
            var, n, mean, sign = (e_squares[:], D, e_shift[:], 1.0) if key == "e" else (
                mv[key][:, :, 1], 1, mv[key][:, :, 0], -1.0)
            if part == 0:
                v.wait_ge(lnexp[key], j * 2 + 2)
                v.scalar_tensor_tensor(a[:, 2, :], var, n * EPS, a[:, 1, :], ALU.add, ALU.mult
                                       ).then_inc(newton[key], 1)
            elif part == 1:
                v.wait_ge(newton[key], j * 4 + 1)
                v.scalar_tensor_tensor(a[:, 3, :], a[:, 2, :], -0.5 / n, a[:, 1, :], ALU.mult, ALU.mult
                                       ).then_inc(newton[key], 1)
            elif part == 2:
                v.wait_ge(newton[key], j * 4 + 2)
                v.scalar_tensor_tensor(a[:, 4, :], a[:, 3, :], 1.5, a[:, 1, :], ALU.add, ALU.mult
                                       ).then_inc(newton[key], 1)
            else:
                v.wait_ge(newton[key], j * 4 + 3)
                v.scalar_tensor_tensor(a[:, 5, :], mean, sign, a[:, 4, :], ALU.mult, ALU.mult
                                       ).then_inc(newton[key], 1)

        @block.scalar
        def _(act):
            act.preload_act_table_set("natural_log_exp_and_others")
            act.wait_ge(init, 5)
            act.dma_start(w1_raw, w1).then_inc(w_in, 16)
            act.dma_start(W[:], wexp).then_inc(w_in, 16)
            act.wait_ge(bias_mm, 1)
            act.activation(attn_bias[:], st_ps[0:1, 0:D], ACT.Copy).then_inc(init_a, 1)

            def normalise(key, first, dst, src, done):
                for c in range(NT):
                    n = first + c
                    act.activation(dst(c), src(c), ACT.Identity, bias=nw[key][:, 5, n:n + 1],
                                   scale=nw[key][:, 4, n:n + 1]).then_inc(done, 1)

            def step(at):
                E_, F, O, Q, W_, R = (at.get(k) for k in "EFOQWR")
                if E_:
                    j, p, r = E_
                    act.wait_ge(xe_in[p], r * 16 + 16)
                    wait(act, newton["e"], j * 4)
                    wait(act, xnT_mm, j - 1)
                    for c in range(NT):
                        act.activation(xn[p][:, c, :], xe[p][:, c, :], ACT.Copy, accum_out=e_sum[:, c:c + 1]
                                       ).then_inc(stat["e"], 1)
                    act.wait_ge(stat["e"], j * 9 + 4)
                    act.activation(e_shift[:], e_sum[:], ACT.Copy, scale=-1 / D).then_inc(stat["e"], 1)
                if F:
                    j, p, r = F
                    act.wait_ge(qk_mm, j + 1)
                    wait(act, soft_sum, j)
                    for k in range(2):
                        act.activation(f_abs[:, k * S:(k + 1) * S], qk_ps[:, k * S:(k + 1) * S], ACT.Abs,
                                       bias=b_qk[:, k:k + 1]).then_inc(soft_a, 1)
                    for k in range(2):
                        act.activation(f_relu[:, k * S:(k + 1) * S], qk_ps[:, k * S:(k + 1) * S], ACT.Relu,
                                       bias=b_qk[:, k:k + 1]).then_inc(soft_a, 1)
                if W_:
                    guess(act, "ar", W_[0])
                if F:
                    act.wait_ge(soft_a, j * 6 + 2)
                    act.activation(f_exp[:], f_abs[:], ACT.Exp, scale=-1.0).then_inc(soft_a, 1)
                    act.wait_ge(soft_a, j * 6 + 5)
                    act.activation(f_ln[:], f_exp[:], ACT.Ln, bias=1.0).then_inc(soft_a, 1)
                    act.wait_ge(v_mm, j + 1)
                    wait(act, outer, (j - 1) * NT)
                    wait(act, state_mm, (j - 1) * (NT - 1))
                    act.activation(vx[p][:].rearrange("p c (h w) -> p c h w", w=DEN)[:, :, :, 0:DH],
                                   xv_ps[:].rearrange("p (c h e) -> p c h e", c=NT, h=H), ACT.Copy).then_inc(v_sb, 1)
                if E_:
                    j, p, r = E_
                    act.wait_ge(stat["e"], j * 9 + 5)
                    for c in range(NT):
                        act.activation(xn[p][:, c, :], xe[p][:, c, :], ACT.Square, bias=e_shift[:, c:c + 1],
                                       accum_out=e_squares[:, c:c + 1]).then_inc(stat["e"], 1)
                if W_:
                    act.wait_ge(newton["ar"], W_[0] * 4 + 4)
                if Q:
                    j, p, r = Q
                    wait(act, x1_done, j)
                    normalise("ar", 0, lambda c: an[:, c, :], lambda c: out_ps[:, c * D:(c + 1) * D], an_done)
                if R:
                    j, p, r = R
                    wait(act, scattered[p], r * 2 * NT * 16)
                    normalise("ar", NT, lambda c: rows[p][:, c, 0:D], lambda c: x1[p][:, c, :], rows_done)
                    act.wait_ge(x2T_mm, j + 1)
                    wait(act, logit_mm, j)
                    act.activation(xn2T[:], out_ps[:], ACT.Copy).then_inc(x2T_sb, 1)
                if E_:
                    guess(act, "e", E_[0])
                if F:
                    j, p, r = F
                    act.wait_ge(qkt_mm, j + 1)
                    wait(act, cum, (j - 1) * NT * 2)
                    wait(act, m_prod, (j - 1) * PRODS[NT])
                    for k in range(2):
                        act.activation(qk[p][:, 2 * k:2 * k + 2, :].rearrange("p c w -> p (c w)"),
                                       qk_ps[:, k * 512:(k + 1) * 512], ACT.Copy).then_inc(qk_sb, 1)
                if O:
                    j, p, r = O
                    act.wait_ge(oT_mm, j + 1)
                    wait(act, a_mm, j)
                    act.activation(oT[:], out_ps[:], ACT.Copy).then_inc(oT_sb, 1)
                if E_:
                    j, p, r = E_
                    act.wait_ge(newton["e"], j * 4 + 4)
                    wait(act, xnT_mm, j - 1)
                    normalise("e", 0, lambda c: xn[p][:, c, :], lambda c: xe[p][:, c, :], xn_done)
                if R:
                    j, p, r = R
                    act.wait_ge(route, j * 13 + 9)
                    wait(act, route, (j - 1) * 13 + 13)
                    act.activation(etop[:], dtop[:], ACT.Exp).then_inc(etop_done, 1)
                if E_:
                    j, p, r = E_
                    act.wait_ge(xnT_mm, j + 1)
                    wait(act, v_mm, j)
                    act.activation(xnT[:], xv_ps[:], ACT.Copy).then_inc(xnT_sb, 1)
            def w1_leading():
                act.wait_ge(w_in, 32)
                for k in range(2):
                    es = slice(k * E // 2, (k + 1) * E // 2)
                    act.activation(w1_parts[:, es, 0, :], w1_raw[:, es, :], ACT.Copy).then_inc(w1_hi, 1)

            run_steps(act, step, w1_leading)

            act.preload_act_table(ACT.Gelu_apprx_tanh)
            def tile(i, q, r):
                p = q % 2
                act.wait_ge(gT_mm, i + 1)
                wait(act, h_mm, (i - 1) * FC)
                act.activation(xgT_hi[p][:], gT_ps[p][:, 0:T], ACT.Copy).then_inc(gT_sb, 1)
                if not (isinstance(i, int) and i == 0):
                    gelu(i - 1, (q - 1) % RING)

            def gelu(i, q):
                p = q % 2
                for f in range(FC):
                    if f % 2 == 0:
                        act.wait_ge(h_mm, i * FC + f + 2)
                    if f == 0:
                        wait(act, y_mm, i - 1)
                    act.activation(hid[p][:, f, :], h_ps(p, f), ACT.Gelu_apprx_tanh,
                                   bias=we[q][:, B1_AT + f:B1_AT + f + 1]).then_inc(h_done, 1)

            run_tiles(act, tile)
            gelu(MOE_TILES - 1, (MOE_TILES - 1) % RING)

            act.preload_act_table_set("natural_log_exp_and_others")

            def scale_first(j, q, r):
                p = q % 2
                act.wait_ge(pc_done, j + 1)
                act.wait_ge(y_in[q], r * 32 + 32)
                wait(act, ys_done, (j - 1) * NT)
                for c in range(NT):
                    act.activation(yp[p][:, c, :], y0[q][:, c, :], ACT.Copy, scale=pc[q][:, 2 * c:2 * c + 1]
                                   ).then_inc(yp_done, 1)

            def last(j, q, r, more=True):
                p = q % 2
                guess(act, "c", j)
                if more:
                    scale_first(j + 2, (q + 2) % RING, r + (q + 2) // RING)
                act.wait_ge(newton["c"], j * 4 + 4)
                wait(act, fin_done, j - 1)
                for c in range(NT):
                    act.activation(yn[p][:, c, :], ys[q][:, c, :], ACT.Identity,
                                   bias=nw["c"][:, 5, c:c + 1], scale=nw["c"][:, 4, c:c + 1]).then_inc(yn_done, 1)

            for j in range(2):
                scale_first(j, j, 0)
            for j in range(RING):
                last(j, j, 0)
            with act.Fori(1, B // RING - 1) as t:
                for q in range(RING):
                    last(RING * t + q, q, t)
            for j in range(B - RING, B):
                last(j, j % RING, j // RING, j < B - 2)

        @block.tensor
        def _(pe):
            pe.wait_ge(consts_in, n_const)
            pe.matmul(st_ps[0:1, 0:D], b_v, w_o, start=True, stop=False)
            pe.wait_ge(init, 5)
            pe.matmul(st_ps[0:1, 0:D], ones_row[0:1, 0:1], b_o, start=False, stop=True).then_inc(bias_mm, 1)
            pe.wait_ge(init_a, 1)

            def prefix(at, c):
                if "M" not in at:
                    return
                j, p, r = at["M"]
                n = j * NT + c
                before = j * PRODS[NT] + PRODS[c]
                qt, kt = qk[p][:, c, 0:D], qk[p][:, c, D:2 * D]
                if c == 0:
                    pe.wait_ge(v_sb, j + 1)
                    pe.wait_ge(qk_sb, j * 2 + 2)
                wait(pe, m_prod, before - 2)
                m = pe.matmul(k1_ps, tri_s, kt, start=True, stop=True)
                if c > 0:
                    wait(pe, state_sb, j * (NT - 1) + c)
                    m = pe.matmul(inter_ps, qkT[p][:, c * P:(c + 1) * P], state[(c - 1) % 2][:], start=True, stop=True)
                m.then_inc(k1_mm, 1)
                pe.wait_ge(outer, n + 1)
                for k in range(2):
                    wait(pe, m_prod, before - 1 + k)
                    pe.matmul(kv_ps[k][:], tri_s, kv[c % 2][:, k * 512:(k + 1) * 512], start=True, stop=True
                              ).then_inc(cum, 1)
                if c < NT - 1:
                    wait(pe, state_sb, j * (NT - 1) + c)
                    if c == 0:
                        wait(pe, slots, (j - OFFSETS["R"] + OFFSETS["M"] - 1) * 7 + 4)
                    pe.matmul(st_ps[:, 0:HV], kt, vx[p][:, c, :], start=(c == 0), stop=True,
                              skip_group_check=True).then_inc(state_mm, 1)

            def step(at):
                E_, F, M, O, R = (at.get(k) for k in "EFMOR")
                if F:
                    j, p, r = F
                    pe.wait_ge(xnT_sb, j + 1)
                    wait(pe, qk_sb, j * 2)
                    for k in range(2):
                        m = pe.matmul(qk_ps[:, k * S:(k + 1) * S], w_qkv[:, k * D:(k + 1) * D], xnT[:],
                                      start=True, stop=True)
                    m.then_inc(qk_mm, 1)
                    for c in range(NT):
                        m = pe.matmul(xv_ps[:, c * D:(c + 1) * D], xnT[:, c * P:(c + 1) * P], w_qkv[:, 2 * D:3 * D],
                                      start=True, stop=True)
                    m.then_inc(v_mm, 1)
                prefix(at, 0)
                prefix(at, 1)
                prefix(at, 2)
                if R:
                    j, p, r = R
                    pe.wait_ge(rows_done, j * NT + NT)
                    wait(pe, an_done, (min(j + 2, B) if isinstance(j, int) else j + 2) * NT)
                    for c in range(NT):
                        m = pe.transpose(out_ps[:, c * P:(c + 1) * P], rows[p][:, c, 0:D], idn)
                    m.then_inc(x2T_mm, 1)
                if F:
                    j, p, r = F
                    pe.wait_ge(soft_sum, j + 1)
                    for c in range(NT):
                        for k in range(2):
                            m = pe.transpose(qk_ps[:, (2 * c + k) * P:(2 * c + k + 1) * P],
                                             qkT[p][:, k * S + c * P:k * S + (c + 1) * P], idn)
                    m.then_inc(qkt_mm, 1)
                if R:
                    j, p, r = R
                    pe.wait_ge(x2T_sb, j + 1)
                    wait(pe, slots, (j - 1) * 7 + 4)
                    if M:
                        pe.wait_ge(state_sb, M[0] * (NT - 1) + NT - 1)
                    for c in range(NT):
                        m = pe.matmul(logit_ps[:, c, :], xn2T[:, c * P:(c + 1) * P], w_gate, start=True, stop=True)
                    m.then_inc(logit_mm, 1)
                if O:
                    j, p, r = O
                    pe.wait_ge(o_done, j + 1)
                    wait(pe, an_done, j * NT)
                    for c in range(NT):
                        m = pe.transpose(out_ps[:, c * P:(c + 1) * P], o[p][:, c, :], idn)
                    m.then_inc(oT_mm, 1)
                prefix(at, 3)
                if E_:
                    j, p, r = E_
                    pe.wait_ge(xn_done, j * NT + NT)
                    wait(pe, v_sb, j)
                    for c in range(NT):
                        m = pe.transpose(xv_ps[:, c * P:(c + 1) * P], xn[p][:, c, :], idn)
                    m.then_inc(xnT_mm, 1)
                if O:
                    j, p, r = O
                    pe.wait_ge(oT_sb, j + 1)
                    for c in range(NT):
                        pe.matmul(out_ps[:, c * D:(c + 1) * D], ones_row[:], attn_bias[:], start=True, stop=False)
                        m = pe.matmul(out_ps[:, c * D:(c + 1) * D], oT[:, c * P:(c + 1) * P], w_o,
                                      start=False, stop=True)
                    m.then_inc(a_mm, 1)
                if R:
                    j, p, r = R
                    pe.wait_ge(route, j * 13 + 12)
                    for c in range(NT):
                        pe.matmul(rank_ps[:, c, :], tri_b[:], hot_b[:, c, :], start=True, stop=(c == 0))
                        for b in range(c):
                            pe.matmul(rank_ps[:, c, :], ones_b[:], hot_b[:, b, :], start=False, stop=(b == c - 1))
                    for c in range(NT):
                        m = pe.matmul(count_ps, ones_b[:], hot_b[:, c, :], start=(c == 0), stop=(c == NT - 1))
                    m.then_inc(rank_mm, 1)

            run_steps(pe, step)

            def rows_T(i, q, r):
                pe.wait_ge(xg_in[q], r * 16 + 16)
                wait(pe, gT_lo, i - 1)
                for k in range(2):
                    m = pe.transpose(gT_ps[q % 2][:, k * P:(k + 1) * P], xg[q][:, k, 0:D], idn)
                m.then_inc(gT_mm, 1)

            def up(i, q):
                p = q % 2
                pe.wait_ge(gT_lo, i + 1)
                pe.wait_ge(we_done, i * 2 + 2)
                wait(pe, h_done, (i - 1) * FC)
                for f in range(FC):
                    w_hi, w_lo = (we1[p][:, k * FF + f * P:k * FF + (f + 1) * P] for k in range(2))
                    pe.matmul(h_ps(p, f), w_hi, xgT_lo[p][:], start=True, stop=False)
                    pe.matmul(h_ps(p, f), w_lo, xgT_hi[p][:], start=False, stop=False)
                    pe.matmul(h_ps(p, f), w_hi, xgT_hi[p][:], start=False, stop=True).then_inc(h_mm, 1)

            def down(i, q):
                p = q % 2
                pe.wait_ge(h_done, i * FC + FC)
                wait(pe, y_done, i - 1)
                for k in range(2):
                    for f in range(FC):
                        m = pe.matmul(y_ps[p][:, k * D:(k + 1) * D], hid[p][:, f, k * P:(k + 1) * P],
                                      we[q][:, f * D:(f + 1) * D], start=(f == 0), stop=(f == FC - 1))
                m.then_inc(y_mm, 1)

            pe.wait_ge(an_done, B * NT)
            pe.wait_ge(x2T_sb, B)
            pe.wait_ge(slots, B * 7)
            pe.wait_ge(m_prod, B * PRODS[NT])

            def tile(i, q, r):
                rows_T(i, q, r)
                if not (isinstance(i, int) and i < 1):
                    up(i - 1, (q - 1) % RING)
                if not (isinstance(i, int) and i < 2):
                    down(i - 2, (q - 2) % RING)

            run_tiles(pe, tile)
            up(MOE_TILES - 1, (MOE_TILES - 1) % RING)
            for i in range(MOE_TILES - 2, MOE_TILES):
                down(i, i % RING)

        @block.vector
        def _(v):
            v.memset(eps_t[:], EPS).then_inc(init, 1)
            v.memset(ones_row[:], 1.0).then_inc(init, 1)
            v.memset(ones_b[:], 1.0).then_inc(init, 1)
            for k in range(2):
                v.memset(vx[k][:].rearrange("p c (h w) -> p (c h) w", w=DEN)[:, :, DH:DEN], 1.0)
            v.memset(rows[0][:, :, D:RW], 0.0)
            v.memset(rows[1][:, :, D:RW], 0.0)
            v.memset(mv["ar"][:], 0.0)
            v.wait_ge(consts_in, n_const)
            v.tensor_copy(tri_b[:], tri_strict).then_inc(init, 1)
            v.tensor_copy(base[:], ecap).then_inc(init, 1)
            v.tensor_copy(token[:], tok0).then_inc(init, 1)
            v.wait_ge(init, 6)

            def k1_product(at, c):
                if "M" not in at:
                    return
                j, p, r = at["M"]
                n = j * NT + c
                v.wait_ge(k1_mm, n + 1)
                wait(v, m_red, n - 1)
                v.tensor_tensor(prod[c % 2][:, :, 0:DH, DH], k1_ps.rearrange("p (h d) -> p h d", h=H),
                                qk[p][:, c, 0:D].rearrange("p (h d) -> p h d", h=H), ALU.mult).then_inc(m_prod, 1)

            def earlier_part(at, c):
                if "M" in at:
                    v.tensor_copy(prod[c % 2][:, :, DH, :], inter_ps.rearrange("p (h w) -> p h w", h=H)
                                  ).then_inc(m_prod, 1)

            def kv_product(at, c, k):
                if "M" not in at:
                    return
                j, p, r = at["M"]
                hs = slice(k * 8, k * 8 + 8)
                v.wait_ge(cum, 2 * (j * NT + c) + k + 1)
                v.tensor_tensor(prod[c % 2][:, hs, 0:DH, 0:DH],
                                kv_ps[k][:].rearrange("p (h d e) -> p h d e", h=8, d=DH),
                                qk[p][:, c, 0:D].rearrange("p (h d) -> p h d", h=H)[:, hs, :, None]
                                .broadcast_to((P, 8, DH, DH)), ALU.mult).then_inc(m_prod, 1)

            def keep_state(at, c):
                if "M" not in at:
                    return
                j, p, r = at["M"]
                v.wait_ge(state_mm, j * (NT - 1) + c + 1)
                v.tensor_tensor(state[c % 2][:], st_ps[:, 0:HV], head_mask, ALU.mult).then_inc(state_sb, 1)

            def summed(at, c):
                if "M" not in at:
                    return
                j, p, r = at["M"]
                v.wait_ge(m_prod, j * PRODS[NT] + PRODS[c + 1])
                parts = DEN if c > 0 else DH
                if c == 0:
                    wait(v, o_done, j)
                v.tensor_reduce(num[:, c], prod[c % 2][:, :, 0:parts, :].rearrange("p h d e -> p h e d"),
                                AX, ALU.add).then_inc(m_red, 1)

            def step(at):
                E_, M, O, Q, W_, R = (at.get(k) for k in "EMOQWR")
                k1_product(at, 0)
                kv_product(at, 0, 0)
                kv_product(at, 0, 1)
                keep_state(at, 0)
                summed(at, 0)
                if W_:
                    newton_part(v, "ar", W_[0], 0)
                k1_product(at, 1)
                if W_:
                    newton_part(v, "ar", W_[0], 1)
                earlier_part(at, 1)
                if W_:
                    newton_part(v, "ar", W_[0], 2)
                kv_product(at, 1, 0)
                if W_:
                    newton_part(v, "ar", W_[0], 3)
                kv_product(at, 1, 1)
                keep_state(at, 1)
                summed(at, 1)
                k1_product(at, 2)
                earlier_part(at, 2)
                kv_product(at, 2, 0)
                kv_product(at, 2, 1)
                keep_state(at, 2)
                summed(at, 2)
                if Q:
                    v.wait_ge(x1_done, Q[0] + 1)
                for c in range(NT):
                    if E_:
                        newton_part(v, "e", E_[0], c)
                    if Q:
                        tile_sums(v, "r", c, x1[Q[1]][:, c, :])
                if R:
                    j, p, r = R
                    n0 = j * 13
                    v.wait_ge(logit_mm, j + 1)
                    v.tensor_copy(logit[:], logit_ps).then_inc(route, 1)
                if R:
                    hold(v, (route, n0 + 1))
                    for c in range(NT):
                        v.max(top[:, c, :], logit[:, c, :]).then_inc(route, 1)
                if Q:
                    means(v, "r", Q[0])
                if R:
                    hold(v, (route, n0 + 5), (etop_done, j))
                    for c in range(NT):
                        m = v.max_index(topi[:, c, :], top[:, c, :], logit[:, c, :])
                        m.then_inc(route if c < NT - 1 else meta, 1)
                    v.tensor_tensor(dtop[:], top[:], top[:, :, 0:1].broadcast_to((P, NT, E)), ALU.subtract
                                    ).then_inc(route, 1)
                    v.wait_ge(meta, j * 4 + 1)
                    v.tensor_copy(topf[:], topi[:, :, 0:2]).then_inc(route, 1)
                    wait(v, scattered[p], r * 2 * NT * 16)
                    v.tensor_copy(rows[p][:, :, D], token[:]).then_inc(meta, 1)
                    v.wait_ge(route, n0 + 10)
                    v.tensor_tensor(hot[:], iota8[:, None, None, :].broadcast_to((P, NT, 2, E)),
                                    topf[:, :, :, None].broadcast_to((P, NT, 2, E)), ALU.is_equal).then_inc(route, 1)
                    v.tensor_copy(rows[p][:, :, D + 1], topf[:, :, 0]).then_inc(meta, 1)
                    v.wait_ge(route, n0 + 11)
                    wait(v, rank_mm, j)
                    v.tensor_tensor(hot_b[:], hot[:, :, 0, :], hot[:, :, 1, :], ALU.add).then_inc(route, 1)
                    v.wait_ge(meta, j * 4 + 3)
                    v.tensor_scalar(token[:], token[:], float(S), None, ALU.add).then_inc(meta, 1)
                k1_product(at, 3)
                earlier_part(at, 3)
                kv_product(at, 3, 0)
                kv_product(at, 3, 1)
                if R:
                    j, p, r = R
                    first = tile_of(v, j)
                    v.wait_ge(etop_done, j + 1)
                    v.tensor_reduce(zsum[:], etop[:], AX, ALU.add).then_inc(slots, 1)
                summed(at, 3)
                if M:
                    v.wait_ge(m_red, M[0] * NT + NT)
                    v.reciprocal(rden[:], num[:, :, :, DH]).then_inc(m_rden, 1)
                if R:
                    v.wait_ge(slots, j * 7 + 1)
                    v.reciprocal(rz[:], zsum[:]).then_inc(slots, 1)
                if M:
                    mj, mp, mr = M
                    v.wait_ge(m_rden, mj + 1)
                    wait(v, oT_mm, mj - 1)
                    v.tensor_tensor(o[mp][:].rearrange("p c (h e) -> p c h e", h=H), num[:, :, :, 0:DH],
                                    rden[:, :, :, None].broadcast_to((P, NT, H, DH)), ALU.mult).then_inc(o_done, 1)
                if R:
                    n0 = j * 7
                    v.wait_ge(rank_mm, j + 1)
                    v.tensor_tensor(pos[:], rank_ps, base[:, None, :].broadcast_to((P, NT, E)), ALU.add
                                    ).then_inc(slots, 1)
                    v.wait_ge(slots, n0 + 2)
                    v.tensor_tensor(prob_all[:, bass.ds(first, NT), :],
                                    etop[:, :, 0:2], rz[:, :, None].broadcast_to((P, NT, 2)), ALU.mult
                                    ).then_inc(route, 1)
                    v.wait_ge(slots, n0 + 3)
                    v.tensor_tensor(base[:], base[:], count_ps, ALU.add).then_inc(slots, 1)
                    v.tensor_tensor(psel[:], hot[:], pos[:, :, None, :].broadcast_to((P, NT, 2, E)), ALU.mult
                                    ).then_inc(slots, 1)
                if O:
                    v.wait_ge(a_mm, O[0] + 1)
                    for c in range(NT):
                        tile_sums(v, "a", c, out_ps[:, c * D:(c + 1) * D])
                if R:
                    v.wait_ge(slots, n0 + 5)
                    v.tensor_reduce(slotf[:].rearrange("p (c k) -> p c k", k=2), psel[:], AX, ALU.add
                                    ).then_inc(slots, 1)
                if O:
                    means(v, "a", O[0])
                if R:
                    v.wait_ge(slots, n0 + 6)
                    wait(v, scattered[p], r * 2 * NT * 16)
                    v.tensor_copy(slot[p][:], slotf[:]).then_inc(slots, 1)

            def w1_rest():
                for k in range(2):
                    es = slice(k * E // 2, (k + 1) * E // 2)
                    v.wait_ge(w1_hi, k + 1)
                    v.tensor_tensor(w1_parts[:, es, 1, :], w1_raw[:, es, :], w1_parts[:, es, 0, :].bitcast(F32),
                                    ALU.subtract).then_inc(w1_lo, 1)

            run_steps(v, step, w1_rest)

            tn = [0]

            def t_op(ins):
                tn[0] += 1
                ins.then_inc(table, 1)
                v.wait_ge(table, tn[0])

            v.wait_ge(slots, B * 7)
            t_op(v.tensor_copy(end_i[:], base[:]))
            t_op(v.tensor_tensor(cnt[:], base[:], ecap, ALU.subtract))
            t_op(v.tensor_tensor(cmp32, cnt[:, :, None].broadcast_to((P, E, 32)),
                                 m256[:, None, :].broadcast_to((P, E, 32)), ALU.is_gt))
            t_op(v.tensor_reduce(ntile[:], cmp32, AX, ALU.add))
            t_op(v.tensor_tensor(trie, lower, ntile[:, None, :].broadcast_to((P, E, E)), ALU.mult))
            t_op(v.tensor_reduce(tend[:], trie, AX, ALU.add))
            t_op(v.tensor_tensor(ge, tnum[:, :, None].broadcast_to((P, MOE_TILES, E)),
                                 tend[:, None, :].broadcast_to((P, MOE_TILES, E)), ALU.is_ge))
            t_op(v.tensor_reduce(ex_of[:], ge, AX, ALU.add))
            t_op(v.tensor_tensor(gen, ge, ntile[:, None, :].broadcast_to((P, MOE_TILES, E)), ALU.mult))
            t_op(v.tensor_reduce(t_start[:], gen, AX, ALU.add))
            t_op(v.tensor_tensor(row_of[:], tnum, t_start[:], ALU.subtract))
            t_op(v.tensor_scalar(row_b[:], row_of[:], float(T), None, ALU.mult))
            t_op(v.scalar_tensor_tensor(row_of[:], ex_of[:], float(CAP), row_b[:], ALU.mult, ALU.add))
            t_op(v.tensor_scalar(row_b[:], row_of[:], float(E * CAP), None, ALU.min))
            t_op(v.tensor_copy(row_i[:], row_b[:]))
            t_op(v.tensor_scalar(ex_min[:], ex_of[:], float(E - 1), None, ALU.min))
            t_op(v.tensor_copy(ex_i[:], ex_min[:]))
            assert tn[0] == TABLE_OPS
            v.wait_ge(w1_lo, 2)

            def tile(i, q, r):
                e = v.value_load(ex_i[0:1, bass.ds(i, 1)], min_val=0, max_val=E - 1)
                hold(v, (y_done, i - RING + 1))
                v.tensor_copy(we[q], W[:, bass.ds(e, 1), :].rearrange("p a w -> p (a w)")).then_inc(we_done, 1)
                if not (isinstance(i, int) and i < 2):
                    hold(v, (h_mm, (i - 1) * FC))
                v.tensor_copy(we1[q % 2][:], w1_parts[:, bass.ds(e, 1), :, :].rearrange("p a k f -> p (a k f)")
                              ).then_inc(we_done, 1)
                v.wait_ge(we_done, i * 2 + 1)
                v.wait_ge(xg_in[q], r * 16 + 16)
                v.tensor_scalar(second[q][:], xg[q][:, :, D + 1], we[q][:, NUMBER_AT:NUMBER_AT + 1], float(N),
                                ALU.not_equal, ALU.mult).then_inc(dest_a, 1)
                v.wait_ge(dest_a, i + 1)
                wait(v, y_sent[q], r * 32)
                v.tensor_tensor(dest[q][:], second[q][:], xg[q][:, :, D], ALU.add).then_inc(dest_done, 1)
                v.wait_ge(gT_sb, i + 1)
                v.tensor_tensor(xgT_lo[q % 2][:], gT_ps[q % 2][:, 0:T], xgT_hi[q % 2][:].bitcast(F32), ALU.subtract
                                ).then_inc(gT_lo, 1)
                if not (isinstance(i, int) and i < 2):
                    finish(i - 2, (q - 2) % RING, r - (q < 2))

            def finish(i, q, r):
                v.wait_ge(y_mm, i + 1)
                wait(v, y_sent[q], r * 32)
                v.tensor_tensor(yv[q][:], y_ps[q % 2][:, 0:T].rearrange("p (k d) -> p k d", k=2),
                                we[q][:, None, B2_AT:B2_AT + D].broadcast_to((P, 2, D)), ALU.add
                                ).then_inc(y_done, 1)

            run_tiles(v, tile)
            for i in range(MOE_TILES - 2, MOE_TILES):
                finish(i, i % RING, i // RING)

            def weights(j, q):
                first = tile_of(v, j)
                hold(v, (ys_done, (j - RING + 1) * NT))
                v.tensor_copy(pc[q][:], prob_all[:, bass.ds(first, NT), :].rearrange("p c k -> p (c k)")
                              ).then_inc(pc_done, 1)

            def last(j, q, r):
                p = q % 2
                v.wait_ge(pc_done, j + 1)
                v.wait_ge(y_in[q], r * 32 + 32)
                wait(v, yn_done, (j - RING + 1) * NT)
                for c in range(NT):
                    v.wait_ge(yp_done, j * NT + c + 1)
                    v.scalar_tensor_tensor(ys[q][:, c, :], y1[q][:, c, :], pc[q][:, 2 * c + 1:2 * c + 2],
                                           yp[p][:, c, :], ALU.mult, ALU.add).then_inc(ys_done, 1)
                v.wait_ge(ys_done, j * NT + NT)
                for c in range(NT):
                    if not (isinstance(j, int) and j == 0):
                        newton_part(v, "c", j - 1, c)
                    tile_sums(v, "c", c, ys[q][:, c, :])
                if not (isinstance(j, int) and j >= B - 2):
                    weights(j + 2, (q + 2) % RING)
                means(v, "c", j, (newton["c"], j * 4))

            for p in range(2):
                v.wait_ge(x1_kept[p], B // 2 * 16)
            weights(0, 0)
            weights(1, 1)
            for j in range(RING):
                last(j, j, 0)
            with v.Fori(1, B // RING - 1) as t:
                for q in range(RING):
                    last(RING * t + q, q, t)
            for j in range(B - RING, B):
                last(j, j % RING, j // RING)
            for part in range(4):
                newton_part(v, "c", B - 1, part)

        @block.gpsimd
        def _(gp):
            gp.wait_ge(init, 6)

            def outer_product(at, c):
                if at:
                    j, p, r = at
                    if c == 0:
                        gp.wait_ge(qk_sb, j * 2 + 2)
                        gp.wait_ge(v_sb, j + 1)
                    wait(gp, cum, (j * NT + c - 1) * 2)
                    gp.tensor_tensor(
                        kv[c % 2][:].rearrange("p (h d e) -> p h d e", h=H, d=DH),
                        qk[p][:, c, D:2 * D].rearrange("p (h d) -> p h d", h=H)[:, :, :, None]
                        .broadcast_to((P, H, DH, DH)),
                        vx[p][:, c, :].rearrange("p (h w) -> p h w", w=DEN)[:, :, None, 0:DH]
                        .broadcast_to((P, H, DH, DH)), ALU.mult).then_inc(outer, 1)

            def scatter(at, choices):
                j, p, r = at
                for n in choices:
                    gp.indirect_dma_start(
                        out=bucket, out_offset=bass.IndirectOffsetOnAxis(ap=slot[p][:, n:n + 1], axis=0),
                        in_=rows[p][:, n // 2, :], in_offset=None).then_inc(scattered[p], 16)

            def step(at):
                F, M, Q, S_ = (at.get(k) for k in "FMQS")
                outer_product(M, 2)
                if F:
                    j, p, r = F
                    gp.wait_ge(soft_a, j * 6 + 6)
                    wait(gp, qkt_mm, j - 1)
                    wait(gp, cum, (j - 1) * NT * 2)
                    gp.tensor_tensor(qkT[p][:], f_ln[:], f_relu[:], ALU.add).then_inc(soft_sum, 1)
                outer_product(M, 3)
                if Q:
                    j, p, r = Q
                    gp.wait_ge(an_done, j * NT + NT)
                    gp.wait_ge(xr_in[p], r * 16 + 16)
                    wait(gp, x1_kept[p], r * 16)
                    wait(gp, rows_done, (j - 1) * NT)
                    gp.tensor_tensor(x1[p][:], an[:], xr[p][:], ALU.add).then_inc(x1_done, 1)
                if S_:
                    hold(gp, (slots, S_[0] * 7 + 7), (meta, S_[0] * 4 + 4), (rows_done, S_[0] * NT + NT))
                    scatter(S_, range(0, 3))
                outer_product(F, 0)
                if S_:
                    scatter(S_, range(3, 6))
                outer_product(F, 1)
                if S_:
                    scatter(S_, range(6, 2 * NT))

            run_steps(gp, step)

            def send(i, q, r):
                hold(gp, (y_done, i + 1), (dest_done, i + 1))
                for k in range(2):
                    gp.indirect_dma_start(
                        out=ychoice, out_offset=bass.IndirectOffsetOnAxis(ap=dest[q][:, k:k + 1], axis=0),
                        in_=yv[q][:, k, :], in_offset=None, bounds_check=2 * N - 1, oob_is_err=False
                    ).then_inc(y_sent[q], 16)

            run_tiles(gp, send)

            for p in range(2):
                gp.wait_ge(x1_kept[p], B // 2 * 16)

            def last(j, p, r):
                first = tile_of(gp, j)
                hold(gp, (yn_done, j * NT + NT), (stored[p], r * 16))
                gp.tensor_tensor(fin[p], yn[p][:], x1_all[:, bass.ds(first, NT), :], ALU.add).then_inc(fin_done, 1)

            for j in range(2):
                last(j, j, 0)
            with gp.Fori(1, B // 2) as t:
                for p in range(2):
                    last(2 * t + p, p, t)


def kernel(**inputs):
    import numpy as np
    import concourse.bacc as bacc
    from concourse.bass_utils import run_bass_kernel_spmd as run

    a = {k.split("_", 1)[1]: np.asarray(v) for k, v in inputs.items()}
    f = np.float32
    w1 = a["ffn_w1"].transpose(2, 1, 0)
    w2 = a["ffn_w2"].reshape(D, E, FC, P).transpose(3, 1, 2, 0).reshape(P, E, FC * D)
    b1 = a["ffn_b1"].reshape(E, FC, P).transpose(2, 0, 1)
    b2 = np.broadcast_to(a["ffn_b2"][None], (P, E, D))
    number = np.zeros((P, E, 2), f)
    number[:, :, 0] = np.arange(E)
    pad = np.zeros((T, RW), f)
    pad[:, D] = N + np.arange(T)
    pad[:, D + 1] = -1
    consts = np.zeros((P, 188), f)
    consts[:, 0:E] = np.arange(E)
    consts[:, E:2 * E] = np.arange(E) * CAP
    consts[:, 16:48] = np.arange(32) * T
    consts[:, 48:112] = np.tril(np.ones((E, E))).reshape(-1)
    consts[:, 112:112 + MOE_TILES] = np.arange(MOE_TILES)
    consts[:, 183:187] = np.arange(P)[:, None] + P * np.arange(NT)[None]
    heads = np.arange(P) // DH
    mask = (heads[:, None] == np.arange(HV)[None] // DEN).astype(f)
    parts = {
        "ident": np.eye(P, dtype=f), "w_qkv": np.concatenate([a["attn_Wq"].T, a["attn_Wk"].T, a["attn_Wv"].T], 1),
        "b_qk": np.stack([a["attn_bq"], a["attn_bk"]], 1), "w_o": a["attn_Wo"].T, "w_gate": a["ffn_gate_w"].T,
        "b_v": a["attn_bv"][:, None], "b_o": np.broadcast_to(a["attn_bo"][None], (P, D)),
        "tri": np.triu(np.ones((P, P), f)), "tri_strict": np.triu(np.ones((P, P), f), 1),
        "mask": mask, "con": consts,
    }
    arrays = {
        "x": a["attn_x"], "params": np.concatenate([parts[k] for k in PARAMS], 1),
        "w1": w1, "wexp": np.concatenate([w2, b1, b2, number], 2), "pad": pad.reshape(P, 2 * RW),
    }
    arrays = {f"in_{k}": np.ascontiguousarray(v) for k, v in arrays.items()}
    nc = bacc.Bacc("TRN2", target_bir_lowering=False, num_devices=1)
    args = [nc.dram_tensor(k, v.shape, mybir.dt.from_np(v.dtype), kind="ExternalInput").ap() for k, v in arrays.items()]
    out = nc.dram_tensor("out_0", (B, S, D), F32, kind="ExternalOutput").ap()
    build(nc, *args, out)
    r = run(nc, [arrays], core_ids=[0])
    return r.results[0]["out_0"]
```
